# Optimizing a Trainium2 kernel written in Bass

```python
import numpy as np
import jax
import jax.numpy as jnp

def _softmax(x, axis=-1):
    return jax.nn.softmax(x, axis=axis)

def _gelu(x):
    return jax.nn.gelu(x, approximate=True)

def _silu(x):
    return jax.nn.silu(x)

def _sigmoid(x):
    return jax.nn.sigmoid(x)

def _layernorm(x, axis=-1, eps=1e-05):
    m = jnp.mean(x, axis=axis, keepdims=True)
    v = jnp.var(x, axis=axis, keepdims=True)
    return (x - m) / jnp.sqrt(v + eps)

def _scatter_add(tgt, idx, src, axis=0):
    return tgt.at[idx].add(src)

def _segment_sum(src, seg, n):
    return jax.ops.segment_sum(src, seg, n)
kernel_name = 'mk_adaln_ffn_d1_seqx_r4_1fe65a'

def setup_inputs(seed: int=0):
    np.random.seed(seed)
    _w = jnp.asarray

    def _rec_inputs():
        import jax
        import jax.numpy as jnp
        _rk = jax.random.key(seed)
        x = 7.22e-05 + 1 * jax.random.normal(jax.random.fold_in(_rk, 1), (16, 256, 512), jnp.float32)
        _lenS = 256 - jax.random.randint(jax.random.fold_in(_rk, 7), (16,), 0, max(1, 256 // 4) + 1, jnp.int32)
        _lenS2 = 256 - jax.random.randint(jax.random.fold_in(_rk, 8), (16,), 0, max(1, 256 // 4) + 1, jnp.int32)
        cond_2048 = jax.random.bernoulli(jax.random.fold_in(_rk, 11), 0.5063, (16, 512)).astype(jnp.float32)
        return (x, cond_2048)
    x, cond_2048 = _rec_inputs()

    def _L0_cond_setup():
        import jax, jax.numpy as jnp
        import numpy as np
        NH = 8
        NEG = -1e+30
        key = jax.random.key(seed)
        k1, k2, k3, k4 = jax.random.split(key, 4)
        B, D, T = (4, 256, 512)
        x = jax.random.normal(k1, (B, D, T), dtype=jnp.float32)
        mask = jax.random.randint(k2, (B, T), 0, 2).astype(jnp.float32)
        lim = float(np.sqrt(6.0 / (D + D)))
        Wq = jax.random.uniform(k3, (D, D), dtype=jnp.float32, minval=-lim, maxval=lim)
        Wo = jax.random.uniform(k4, (D, D), dtype=jnp.float32, minval=-lim, maxval=lim)
        return {'x': x, 'mask': mask, 'Wq': Wq, 'Wo': Wo}
    _L0_cond_all = _L0_cond_setup()
    _L0_cond_in = {k: v for k, v in _L0_cond_all.items() if k in ('Wq', 'Wo')}
    del _L0_cond_all

    def _L0_ffn_setup():
        import jax, jax.numpy as jnp
        import numpy as np
        B, S, H = (2, 256, 512)
        E, K = (8, 2)
        I = 352
        IS = 1408
        WSCALE = 0.02
        key = jax.random.key(seed)
        ks = jax.random.split(key, 9)
        f32 = jnp.float32
        return {'hidden_states': jax.random.normal(ks[0], (B, S, H), dtype=f32), 'gate_w': jax.random.normal(ks[1], (E, H), dtype=f32) * WSCALE, 'w_gate': jax.random.normal(ks[2], (E, H, I), dtype=f32) * WSCALE, 'w_up': jax.random.normal(ks[3], (E, H, I), dtype=f32) * WSCALE, 'w_down': jax.random.normal(ks[4], (E, I, H), dtype=f32) * WSCALE, 'sw_gate': jax.random.normal(ks[5], (H, IS), dtype=f32) * WSCALE, 'sw_up': jax.random.normal(ks[6], (H, IS), dtype=f32) * WSCALE, 'sw_down': jax.random.normal(ks[7], (IS, H), dtype=f32) * WSCALE, 'shared_gate_w': jax.random.normal(ks[8], (H, 1), dtype=f32) * WSCALE}
    _L0_ffn_all = _L0_ffn_setup()
    _L0_ffn_in = {k: v for k, v in _L0_ffn_all.items() if k in ('gate_w', 'w_gate', 'w_up', 'w_down', 'sw_gate', 'sw_up', 'sw_down', 'shared_gate_w')}
    del _L0_ffn_all
    return {'x': x, 'cond_2048': cond_2048, 'L0_cond_Wq': _L0_cond_in['Wq'], 'L0_cond_Wo': _L0_cond_in['Wo'], 'L0_ffn_gate_w': _L0_ffn_in['gate_w'], 'L0_ffn_w_gate': _L0_ffn_in['w_gate'], 'L0_ffn_w_up': _L0_ffn_in['w_up'], 'L0_ffn_w_down': _L0_ffn_in['w_down'], 'L0_ffn_sw_gate': _L0_ffn_in['sw_gate'], 'L0_ffn_sw_up': _L0_ffn_in['sw_up'], 'L0_ffn_sw_down': _L0_ffn_in['sw_down'], 'L0_ffn_shared_gate_w': _L0_ffn_in['shared_gate_w']}

def reference(x, cond_2048, L0_cond_Wq, L0_cond_Wo, L0_ffn_gate_w, L0_ffn_w_gate, L0_ffn_w_up, L0_ffn_w_down, L0_ffn_sw_gate, L0_ffn_sw_up, L0_ffn_sw_down, L0_ffn_shared_gate_w):
    import jax
    import jax.numpy as jnp

    def _L0_cond_ref(x, mask, Wq, Wo):
        import jax, jax.numpy as jnp
        import numpy as np
        NH = 8
        NEG = -1e+30
        B, D, T = x.shape
        dk = D // NH
        scale = 1.0 / jnp.sqrt(jnp.asarray(dk, x.dtype))
        xt = jnp.transpose(x, (0, 2, 1))
        q = xt @ Wq.T
        qh = q.reshape(B, T, NH, dk).transpose(0, 2, 1, 3)
        scores = scale * jnp.einsum('bhqd,bhkd->bhqk', qh, qh)
        cmask = mask[:, None, None, :]
        rmask = mask[:, None, :, None]
        logits = (scores * cmask + (1.0 - cmask) * NEG) * rmask
        attn = jax.nn.softmax(logits, axis=-1)
        ctx = jnp.einsum('bhqk,bhkd->bhqd', attn, qh)
        ctx = ctx.transpose(0, 2, 1, 3).reshape(B, T, D)
        out = ctx @ Wo.T
        return jnp.transpose(out, (0, 2, 1))

    def _L0_ffn_ref(hidden_states, gate_w, w_gate, w_up, w_down, sw_gate, sw_up, sw_down, shared_gate_w):
        import jax, jax.numpy as jnp
        import numpy as np
        B, S, H = (2, 256, 512)
        E, K = (8, 2)
        I = 352
        IS = 1408
        WSCALE = 0.02
        x = hidden_states
        logits = jnp.einsum('bsh,eh->bse', x, gate_w)
        probs = jax.nn.softmax(logits, axis=-1)
        top_w, top_i = jax.lax.top_k(probs, K)
        top_w = top_w / jnp.sum(top_w, axis=-1, keepdims=True)
        onehot = jax.nn.one_hot(top_i, E, dtype=x.dtype)
        combine = jnp.einsum('bsk,bske->bse', top_w, onehot)
        g = jnp.einsum('bsh,ehi->besi', x, w_gate)
        u = jnp.einsum('bsh,ehi->besi', x, w_up)
        h = jax.nn.silu(g) * u
        expert_out = jnp.einsum('besi,eih->besh', h, w_down)
        moe_out = jnp.einsum('besh,bse->bsh', expert_out, combine)
        sh = jax.nn.silu(x @ sw_gate) * (x @ sw_up)
        shared_out = sh @ sw_down
        shared_gate = jax.nn.sigmoid(x @ shared_gate_w)
        return moe_out + shared_out * shared_gate
    x = x + _L0_ffn_ref(_L0_cond_ref(x, cond_2048, L0_cond_Wq, L0_cond_Wo), L0_ffn_gate_w, L0_ffn_w_gate, L0_ffn_w_up, L0_ffn_w_down, L0_ffn_sw_gate, L0_ffn_sw_up, L0_ffn_sw_down, L0_ffn_shared_gate_w)
    return x

_drawn_inputs = setup_inputs


def setup_inputs(seed=0):
    import zlib

    import numpy as np

    out = dict(_drawn_inputs(seed))
    spreads = {}
    factors = {}
    for name, (base, spread) in spreads.items():
        noise = np.random.default_rng([zlib.crc32(name.encode()), seed]).standard_normal(out[name].shape)
        drawn = base * np.exp(spread * noise) if base else spread * noise
        out[name] = jnp.asarray(drawn.astype(out[name].dtype))
    for name, factor in factors.items():
        out[name] = (out[name] * factor).astype(out[name].dtype)
    return out
```

```python
def attention(nc, ctx, sems, keep, x, mask, wqT, woT, gates, attn):
    import concourse.bass as bass
    from concourse import mybir

    f32, f32r = mybir.dt.float32, mybir.dt.float32r
    ALU, ACT, AX = mybir.AluOpType, mybir.ActivationFunctionType, mybir.AxisListType

    NB, D, T = x.shape
    P = 128
    NH = 8
    DK = D // NH
    HG = P // DK
    UPB = NH // HG
    NU = NB * UPB
    KT = D // P
    KB = T // P
    SCALE = float(DK) ** -0.5
    NEG = -1e30
    MASKROW = 3 * DK
    MAXROW = MASKROW + 1
    STK = MAXROW + 1
    RING = 4
    STACK_DMAS = 8
    PARTS = 4

    def sb(name, shape, dt):
        return ctx.enter_context(nc.sbuf_tensor(name, shape, dt))

    def bank(name):
        return ctx.enter_context(nc.psum_tensor(name, [P, 512], f32))

    def sem(name):
        return sems.enter_context(nc.semaphore(name))

    wq_f = sb("wq_f", [P, KT, D], f32)
    wq_hi, wq_lo = sb("wq_hi", [P, KT, D], f32r), sb("wq_lo", [P, KT, D], f32r)
    wo_f = sb("wo_f", [P, KT, D], f32)
    wo_hi, wo_lo = sb("wo_hi", [P, KT, D], f32r), sb("wo_lo", [P, KT, D], f32r)
    ident = sb("ident", [P, P], f32)
    ones = sb("ones", [P, DK], f32)
    one_row = sb("one_row", [1, T], f32r)
    NE = gates.shape[1]
    gate_w = sb("gate_w", [P, KB, NE], f32)
    xo_t = [sb(f"xo_t{n}", [P, KB, P], f32) for n in range(2)]
    x_f = [sb(f"x_f{n}", [P, KT, T], f32) for n in range(2)]
    x_hi, x_lo = sb("x_hi", [P, KT, T], f32r), sb("x_lo", [P, KT, T], f32r)
    mask_b = [sb(f"mask_b{n}", [P, T], f32) for n in range(2)]
    row_mask = [sb(f"row_mask{n}", [1, T], f32r) for n in range(2)]
    row_neg = [sb(f"row_neg{n}", [1, T], f32r) for n in range(2)]
    q_f = [sb(f"q_f{n}", [P, T], f32) for n in range(2)]
    q_hi = [sb(f"q_hi{n}", [P, T], f32r) for n in range(2)]
    q_lo = [sb(f"q_lo{n}", [P, T], f32r) for n in range(2)]
    qm_hi = [sb(f"qm_hi{n}", [P, T], f32r) for n in range(2)]
    qm_lo = [sb(f"qm_lo{n}", [P, T], f32r) for n in range(2)]
    kside = [sb(f"kside{n}", [STK, HG, T], f32r) for n in range(RING)]
    qside = [sb(f"qside{n}", [STK, HG, T], f32r) for n in range(RING)]
    v = [sb(f"v{n}", [P, KB, HG, DK], f32) for n in range(RING)]
    maxcol = [sb(f"maxcol{n}", [P, HG * KB], f32) for n in range(2)]
    maxrow = [sb(f"maxrow{n}", [HG * KB, P], f32r) for n in range(2)]
    e = [sb(f"e{n}", [P, HG, T], f32) for n in range(2)]
    num = [sb(f"num{n}", [P, T], f32) for n in range(2)]
    den = [sb(f"den{n}", [P, T], f32) for n in range(2)]
    rden = sb("rden", [P, T], f32)
    c_f = [sb(f"c_f{n}", [P, T], f32) for n in range(2)]
    c_hi = [sb(f"c_hi{n}", [P, T], f32r) for n in range(2 * UPB)]
    c_lo = [sb(f"c_lo{n}", [P, T], f32r) for n in range(2 * UPB)]
    xo = [sb(f"xo{n}", [P, T], f32) for n in range(2)]

    ps_e = [bank(f"ps_e{n}") for n in range(2)]
    ps_m = [bank(f"ps_m{n}") for n in range(2)]
    ps_num, ps_den = bank("ps_num"), bank("ps_den")
    ps_q, ps_o = bank("ps_q"), bank("ps_o")

    one_f = sb("one_f", [1, T], f32)
    w_in = sem("w_in")
    gate_in, xt_mm, xt_done, lg_mm, lg_done = (sem(n) for n in ("gate_in", "xt_mm", "xt_done", "lg_mm", "lg_done"))
    ident_zero = sem("ident_zero")
    ql_done, dve_set = sem("ql_done"), sem("dve_set")
    setup = sem("setup")
    ones_in = sem("ones_in")
    w_split = sem("w_split")
    x_in = [sem(f"x_in{n}") for n in range(2)]
    mask_in = [sem(f"mask_in{n}") for n in range(2)]
    stack_in = [sem(f"stack_in{n}") for n in range(RING)]
    maxrow_in = [sem(f"maxrow_in{n}") for n in range(RING)]
    stored = [sem(f"stored{n}") for n in range(2)]
    e_mm, m_mm, pv_mm = sem("e_mm"), sem("m_mm"), sem("pv_mm")
    q_mm, v_mm, mt_mm, o_mm = sem("q_mm"), sem("v_mm"), sem("mt_mm"), sem("o_mm")
    e_done, q_done, v_done, mt_done = sem("e_done"), sem("q_done"), sem("v_done"), sem("mt_done")
    nd_done, chi_done, o_done = sem("nd_done"), sem("chi_done"), sem("o_done")
    max_done, c_done, rd_done, rows_done = sem("max_done"), sem("c_done"), sem("rd_done"), sem("rows_done")
    xhi_done, x_split, q_split, c_split = sem("xhi_done"), sem("x_split"), sem("q_split"), sem("c_split")

    def words(ap):
        return ap.bitcast(f32)

    def upto(eng, s, value):
        if not (isinstance(value, int) and value <= 0):
            eng.wait_ge(s, value)

    def alone(eng, s, value, met, met_value):
        if not isinstance(value, int):
            value = eng.to_reg(value)
            eng.wait_ge(met, met_value)
        eng.wait_ge(s, value)

    LOOP_UNITS = RING
    NI = NU // LOOP_UNITS

    def run_units(eng, step, before, after):
        for n in range(before, 0):
            step(-1, RING + n)
        for n in range(LOOP_UNITS):
            step(0, n)
        if NI > 3:
            with eng.Fori(1, NI - 2) as i:
                for n in range(LOOP_UNITS):
                    step(i, n)
        for i in range(max(NI - 2, 1), NI):
            for n in range(LOOP_UNITS):
                step(i, n)
        for n in range(after):
            step(NI, n)

    def known(i, n, off=0, lo=0, hi=NU):
        if isinstance(i, int):
            return lo <= RING * i + n + off < hi
        return True

    block = ctx.enter_context(nc.Block())

    @block.sync
    def _(sp):
        sp.dma_start(gate_w[:], gates.rearrange("(k p) e -> p k e", p=P)).then_inc(gate_in, 16)
        sp.dma_start(wq_f[:], wqT.rearrange("(k p) c -> p k c", p=P)).then_inc(w_in, 16)
        sp.dma_start(wo_f[:], woT.rearrange("(k p) c -> p k c", p=P)).then_inc(w_in, 16)

        def load_x(b, par, seen):
            upto(sp, q_split, UPB * (b - 1))
            upto(sp, rows_done, 2 * (b - 1))
            upto(sp, x_split, b - 1)
            sp.dma_start(x_f[par][:], x[bass.ds(b, 1), :, :].rearrange("b (k p) t -> p (b k) t", p=P)).then_inc(x_in[par], 16)
            sp.dma_start(mask_b[par][:], mask[bass.ds(b, 1), :].to_broadcast([P, T])).then_inc(mask_in[par], 16)

        load_x(0, 0, 0)
        load_x(1, 1, 0)
        sp.wait_ge(setup, 3)
        for n in range(RING):
            sp.dma_start(words(kside[n][MAXROW:STK, :, :]), words(one_row[0:1, :]).rearrange("p (a t) -> p a t", a=1).to_broadcast([1, HG, T])).then_inc(ones_in, 16)

        def step(i, n):
            u = RING * i + n
            if known(i, n, 3):
                w, slot, par = u + 3, (n + 3) % RING, (n + 3) % 2
                b = 2 * i + (n + 3) // 2
                bp = (n + 3) // 2 % 2
                alone(sp, q_split, w + 1, w_in, 32)
                upto(sp, rows_done, 2 * (b + 1))
                upto(sp, e_mm, (w - RING + 1) * KB * HG)
                for k, (dst, src) in enumerate(((kside, q_hi), (kside, q_hi), (kside, q_lo),
                                                (qside, qm_hi), (qside, qm_lo), (qside, qm_hi))):
                    k = k % 3
                    sp.dma_start(words(dst[slot][k * DK:(k + 1) * DK, :, :]), words(src[par][:, :])).then_inc(stack_in[slot], 16)
                for dst, src in ((kside, row_neg), (qside, row_mask)):
                    sp.dma_start(words(dst[slot][MASKROW:MAXROW, :, :]),
                                 words(src[bp][0:1, :]).rearrange("p (a t) -> p a t", a=1).to_broadcast([1, HG, T])).then_inc(stack_in[slot], 16)
            if known(i, n, 1):
                w, slot, par = u + 1, (n + 1) % RING, (n + 1) % 2
                upto(sp, mt_done, w + 1)
                upto(sp, e_mm, (w - RING + 1) * KB * HG)
                sp.dma_start(words(qside[slot][MAXROW:STK, :, :]), words(maxrow[par][:, :])).then_inc(maxrow_in[slot], 16)
            if n % 2 == 1:
                if known(i, n, 7):
                    load_x(2 * i + (n + 7) // 2, (n + 7) // 2 % 2, 0)
                if known(i, n, -3, hi=NU):
                    for half in range(KT):
                        b = 2 * i + (n - 3) // 2
                        upto(sp, o_done, KT * b + half + 1)
                        sp.dma_start(attn[bass.ds(b * D + half * P, P), :], xo[half][:, :]).then_inc(stored[half], 16)

        run_units(sp, step, -4, 4)
        for half in range(KT):
            sp.wait_ge(stored[half], 16 * NB)

    @block.gpsimd
    def _(pool):
        pool.memset(ident[:], 0.0).then_inc(ident_zero, 1)
        pool.memset(ones[:], 1.0).then_inc(setup, 1)
        pool.wait_ge(ident_zero, 1)
        pool.affine_select(out=ident[:], in_=ident[:], compare_op=ALU.not_equal, fill=1.0, base=0,
                           pattern=[[-1, P]], channel_multiplier=1).then_inc(setup, 1)

        def step(i, n):
            u = RING * i + n
            if known(i, n, -2):
                w, slot = u - 2, (n - 2) % RING
                upto(pool, chi_done, w + 1)
                pool.tensor_tensor(c_lo[slot][:], c_f[n % 2][:], c_hi[slot][:], ALU.subtract).then_inc(c_split, 1)
            if known(i, n, 4):
                w, par, bp = u + 4, n % 2, n // 2
                upto(pool, q_done, 2 * (w + 1))
                pool.wait_ge(mask_in[bp], 16 * (i + 2))
                if known(i, n, 2):
                    upto(pool, stack_in[(n + 2) % RING], 16 * STACK_DMAS * (i + 1 + (n + 2) // RING))
                pool.tensor_tensor(q_lo[par][:], q_f[par][:], q_hi[par][:], ALU.subtract).then_inc(ql_done, 1)
                pool.tensor_tensor(qm_hi[par][:], q_hi[par][:], mask_b[bp][:], ALU.mult).then_inc(ql_done, 1)
                upto(pool, ql_done, 2 * (w + 1))
                pool.tensor_tensor(qm_lo[par][:], q_lo[par][:], mask_b[bp][:], ALU.mult).then_inc(q_split, 1)
            if n % 2 == 1 and known(i, n, 5):
                w = 2 * i + (n + 5) // 2
                bp = (n + 5) // 2 % 2
                pool.wait_ge(x_in[bp], 16 * (i + (n + 5) // 4 + 1))
                if not (isinstance(w, int) and w <= 0):
                    alone(pool, q_mm, UPB * w, ident_zero, 1)
                pool.tensor_copy(x_hi[:], x_f[bp][:]).then_inc(xhi_done, 1)
                pool.wait_ge(xhi_done, w + 1)
                pool.tensor_tensor(x_lo[:], x_f[bp][:], x_hi[:], ALU.subtract).then_inc(x_split, 1)

        pool.wait_ge(x_in[0], 16)
        pool.tensor_copy(x_hi[:], x_f[0][:]).then_inc(xhi_done, 1)
        pool.wait_ge(xhi_done, 1)
        pool.tensor_tensor(x_lo[:], x_f[0][:], x_hi[:], ALU.subtract).then_inc(x_split, 1)
        run_units(pool, step, -4, 2)

    @block.scalar
    def _(act):
        def step(i, n):
            u = RING * i + n
            for kb in range(KB):
                k = KB * u + kb
                if kb == 1 and known(i, n, -1):
                    w, par = u - 1, (n - 1) % 2
                    act.wait_ge(pv_mm, KB * (w + 1))
                    upto(act, c_done, w - 1)
                    act.activation(den[par][:], ps_den[:, :], ACT.Copy).then_inc(nd_done, 1)
                    act.activation(num[par][:], ps_num[:, :], ACT.Copy).then_inc(nd_done, 1)
                if known(i, n):
                    for g in range(HG):
                        tile = HG * k + g
                        if g == 0:
                            upto(act, pv_mm, k - 1)
                        act.wait_ge(e_mm, tile + 1)
                        act.activation(e[kb % 2][:, g, :], ps_e[g % 2][:, :], ACT.Exp, scale=SCALE).then_inc(e_done, 1)
                if kb == 0 and known(i, n, -2):
                    w, slot = u - 2, (n - 2) % RING
                    act.wait_ge(c_done, w + 1)
                    upto(act, o_mm, KT * (2 * i + (n - 2) // 2 - 1))
                    act.activation(c_hi[slot][:], c_f[n % 2][:], ACT.Copy).then_inc(chi_done, 1)
                if kb == 0 and known(i, n, 1):
                    w, par = u + 1, (n + 1) % 2
                    act.wait_ge(mt_mm, w + 1)
                    if known(i, n, -1):
                        act.wait_ge(maxrow_in[(n - 1) % RING], 16 * (i + (n - 1) // RING + 1))
                    act.activation(maxrow[par][:, :], ps_o[0:HG * KB, 0:P], ACT.Copy, scale=-1.0).then_inc(mt_done, 1)
                if kb == 1 and known(i, n, 3):
                    w, slot = u + 3, (n + 3) % RING
                    act.wait_ge(v_mm, w + 1)
                    upto(act, pv_mm, KB * (w - RING + 1))
                    act.activation(v[slot][:].rearrange("p k g d -> p k d g"),
                                   ps_q[:, :].rearrange("p (k d g) -> p k d g", k=KB, g=HG), ACT.Copy).then_inc(v_done, 1)
                if kb == 2 and known(i, n, 4):
                    w, par = u + 4, n % 2
                    act.wait_ge(q_mm, w + 1)
                    upto(act, v_mm, w - 1)
                    upto(act, q_split, w - 1)
                    if known(i, n, 2):
                        act.wait_ge(stack_in[(n + 2) % RING], 16 * STACK_DMAS * (i + 1 + (n + 2) // RING))
                    act.activation(q_f[par][:], ps_q[:, :], ACT.Copy).then_inc(q_done, 1)
                    act.activation(q_hi[par][:], ps_q[:, :], ACT.Copy).then_inc(q_done, 1)
                if kb >= 2 and n % 2 == 1 and known(i, n, -3, hi=NU):
                    b, half = 2 * i + (n - 3) // 2, kb - 2
                    act.wait_ge(o_mm, KT * b + half + 1)
                    upto(act, stored[half], 16 * b)
                    upto(act, xt_mm, KT * (b - 1) + half + 1)
                    act.activation(xo[half][:], ps_o[:, :], ACT.Copy).then_inc(o_done, 1)

                if kb in (1, 2) and n % 2 == 0 and known(i, n, -4, hi=NU):
                    b, half = 2 * i + (n - 4) // 2, kb - 1
                    act.wait_ge(xt_mm, KT * b + half + 1)
                    upto(act, lg_mm, b)
                    act.activation(xo_t[half][:].rearrange("p k d -> p (k d)"), ps_o[:, :], ACT.Copy).then_inc(xt_done, 1)

        run_units(act, step, -4, 5)

    @block.vector
    def _(dve):
        def normalise(i, n, at):
            w, par = RING * i + n - 1, (n - 1) % 2
            if at < 0:
                return
            if at < PARTS:
                c = slice(at * T // PARTS, (at + 1) * T // PARTS)
                if at == 0:
                    dve.wait_ge(nd_done, 2 * w + 1)
                    upto(dve, c_done, w)
                dve.reciprocal(rden[:, c], den[par][:, c]).then_inc(rd_done, 1)
            elif at == PARTS:
                dve.wait_ge(rd_done, PARTS * (w + 1))
                dve.wait_ge(nd_done, 2 * w + 2)
                upto(dve, c_split, w - 1)
                dve.tensor_tensor(c_f[par][:], num[par][:], rden[:], ALU.mult).then_inc(c_done, 1)

        dve.memset(one_f[:], 1.0).then_inc(dve_set, 1)
        dve.wait_ge(dve_set, 1)
        dve.tensor_copy(one_row[:], one_f[:]).then_inc(setup, 1)
        dve.wait_ge(w_in, 32)
        dve.tensor_copy(wq_hi[:], wq_f[:]).then_inc(w_split, 1)
        dve.tensor_copy(wo_hi[:], wo_f[:]).then_inc(w_split, 1)
        dve.wait_ge(w_split, 2)
        dve.tensor_tensor(wq_lo[:], wq_f[:], wq_hi[:], ALU.subtract).then_inc(w_split, 1)
        dve.tensor_tensor(wo_lo[:], wo_f[:], wo_hi[:], ALU.subtract).then_inc(w_split, 1)

        def step(i, n):
            u = RING * i + n
            if n % 2 == 0 and known(i, n, 4):
                b, bp = 2 * i + (n + 4) // 2, n // 2
                dve.wait_ge(mask_in[bp], 16 * (i + 2))
                if known(i, n, 1):
                    dve.wait_ge(stack_in[(n + 1) % RING], 16 * STACK_DMAS * (i + (n + 1) // RING + 1))
                dve.tensor_copy(row_mask[bp][:], mask_b[bp][0:1, :]).then_inc(rows_done, 1)
                dve.tensor_scalar(row_neg[bp][:], mask_b[bp][0:1, :], -NEG, NEG, ALU.mult, ALU.add).then_inc(rows_done, 1)
            for kb in range(KB):
                if known(i, n, 2):
                    w, par = u + 2, n % 2
                    for g in range(HG):
                        dve.wait_ge(m_mm, (KB * w + kb) * HG + g + 1)
                        if kb == 0 and g == 0:
                            upto(dve, mt_mm, w - 1)
                        dve.reduce_max(maxcol[par][:, g * KB + kb:g * KB + kb + 1], ps_m[g % 2][:, :], AX.X).then_inc(max_done, 1)
                        if g % 2 == 1 and known(i, n, -1):
                            normalise(i, n, 2 * kb + g // 2 - 3)
                elif known(i, n, -1):
                    for at in (2 * kb - 3, 2 * kb - 2):
                        normalise(i, n, at)
                if kb == 3 and n % 2 == 0 and known(i, n, -4, hi=NU):
                    b = 2 * i + (n - 4) // 2
                    dve.wait_ge(lg_mm, b + 1)
                    dve.tensor_copy(keep["logits"][:, bass.ds(KT * b, KT), :],
                                    ps_o[:, 0:KT * NE].rearrange("p (h e) -> p h e", h=KT)).then_inc(lg_done, 1)

        run_units(dve, step, -4, 5)

    @block.tensor
    def _(pe):
        pe.wait_ge(w_split, 4)
        pe.wait_ge(gate_in, 16)
        pe.wait_ge(setup, 3)
        pe.wait_ge(ones_in, 16 * RING)

        def parts(out, a, b, cols, rhs_cols, kt):
            terms = [(t, l, r) for t in range(kt) for l, r in ((a[0], b[0]), (a[0], b[1]), (a[1], b[0]))]
            for m, (t, l, r) in enumerate(terms):
                last = nc.tensor.matmul(out, l(t), r(t), start=(m == 0), stop=(m == len(terms) - 1))
            return last

        def pv(u, n, kb, part):
            slot = n % RING
            if part == 0:
                if kb == 0:
                    upto(pe, nd_done, 2 * u)
                    upto(pe, v_done, u + 1)
                pe.wait_ge(e_done, (KB * u + kb + 1) * HG)
            for g in range(HG):
                rows = slice(g * DK, (g + 1) * DK)
                out, w = ((ps_num, v[slot][:, kb, g, :]), (ps_den, ones[:, :]))[part]
                last = nc.tensor.matmul(out[rows, :], w, e[kb % 2][:, g, :], start=(kb == 0), stop=(kb == KB - 1))
            if part:
                last.then_inc(pv_mm, 1)

        def step(i, n):
            u = RING * i + n
            for kb in range(KB):
                cols = slice(kb * P, (kb + 1) * P)
                if kb == 0 and known(i, n):
                    pe.wait_ge(maxrow_in[n % RING], 16 * (i + 1))
                if kb == 0 and known(i, n, 2):
                    pe.wait_ge(stack_in[(n + 2) % RING], 16 * STACK_DMAS * (i + 1 + (n + 2) // RING))
                before = ((u - 1, n - 1, KB - 1) if known(i, n, -1) else None) if kb == 0 else ((u, n, kb - 1) if known(i, n) else None)
                for g in range(HG):
                    if known(i, n):
                        tile = (KB * u + kb) * HG + g
                        upto(pe, e_done, tile - 1)
                        nc.tensor.matmul(ps_e[g % 2][:, :], kside[n][:, g, cols], qside[n][:, g, :], start=True, stop=True).then_inc(e_mm, 1)
                    if known(i, n, 2):
                        s2 = (n + 2) % RING
                        tile = (KB * (u + 2) + kb) * HG + g
                        upto(pe, max_done, tile - 1)
                        nc.tensor.matmul(ps_m[g % 2][:, :], qside[s2][0:MAXROW, g, cols], kside[s2][0:MAXROW, g, :], start=True, stop=True).then_inc(m_mm, 1)
                    if g % 2 == 1 and before:
                        pv(*before, g // 2)
                if kb == 0 and known(i, n, 1):
                    w = u + 1
                    upto(pe, max_done, (w + 1) * KB * HG)
                    if n % 2 == 0:
                        upto(pe, o_done, KT * (2 * i + (n - 4) // 2 + 1))
                    else:
                        upto(pe, lg_done, 2 * i + (n - 5) // 2 + 1)
                    nc.tensor.transpose(ps_o[0:HG * KB, 0:P], maxcol[(n + 1) % 2][:, :], ident[:, :]).then_inc(mt_mm, 1)
                if kb in (1, 2) and n % 2 == 0 and known(i, n, -4, hi=NU):
                    b, half = 2 * i + (n - 4) // 2, kb - 1
                    upto(pe, o_done, KT * (b + 1))
                    if half == 0 and known(i, n, 1):
                        pe.wait_ge(mt_done, u + 2)
                    upto(pe, xt_done, KT * b + half)
                    for k in range(KB):
                        last = nc.tensor.transpose(ps_o[:, k * P:(k + 1) * P], xo[half][:, k * P:(k + 1) * P], ident[:, :])
                    last.then_inc(xt_mm, 1)
                if kb == 3 and n % 2 == 0 and known(i, n, -4, hi=NU):
                    b = 2 * i + (n - 4) // 2
                    pe.wait_ge(xt_done, KT * (b + 1))
                    for half in range(KT):
                        for k in range(KB):
                            last = nc.tensor.matmul(ps_o[:, half * NE:(half + 1) * NE], xo_t[half][:, k, :], gate_w[:, k, :],
                                                    start=(k == 0), stop=(k == KB - 1))
                    last.then_inc(lg_mm, 1)
                if kb == 1 and known(i, n, 3):
                    w, par = u + 3, (n + 3) % 2
                    pe.wait_ge(q_done, 2 * (w + 1))
                    for k in range(KB):
                        last = nc.tensor.transpose(ps_q[:, k * P:(k + 1) * P], q_f[par][:, k * P:(k + 1) * P], ident[:, :])
                    last.then_inc(v_mm, 1)
                if kb == 2 and known(i, n, 4):
                    w = u + 4
                    hg = n % UPB
                    upto(pe, x_split, 2 * i + (n + 4) // 2 + 1)
                    upto(pe, v_done, w)
                    c = slice(hg * P, (hg + 1) * P)
                    parts(ps_q[:, :], (lambda t: wq_hi[:, t, c], lambda t: wq_lo[:, t, c]),
                          (lambda t: x_hi[:, t, :], lambda t: x_lo[:, t, :]), None, None, KT).then_inc(q_mm, 1)
                if kb >= 2 and n % 2 == 1 and known(i, n, -3, hi=NU):
                    b, half = 2 * i + (n - 3) // 2, kb - 2
                    upto(pe, c_split, UPB * (b + 1))
                    upto(pe, o_done, KT * b + half)
                    if known(i, n, 1):
                        pe.wait_ge(mt_done, u + 2)
                    upto(pe, lg_done, b)
                    c = slice(half * P, (half + 1) * P)
                    s = (n - 3) // 2 % 2 * UPB
                    parts(ps_o[:, :], (lambda t: wo_hi[:, t, c], lambda t: wo_lo[:, t, c]),
                          (lambda t: c_hi[s + t][:, :], lambda t: c_lo[s + t][:, :]), None, None, KT).then_inc(o_mm, 1)

        run_units(pe, step, -4, 5)


def experts(nc, ctx, sems, keep, attn, w_gate, w_up, w_down, routed):
    import concourse.bass as bass
    from concourse import mybir

    f32, f32r, u32 = mybir.dt.float32, mybir.dt.float32r, mybir.dt.uint32
    ALU, ACT, AX = mybir.AluOpType, mybir.ActivationFunctionType, mybir.AxisListType
    P = 128
    NE, H, I = w_gate.shape
    HT = H // P
    ST = keep["slot_tile"]
    SB = ST // P
    NTILES = routed.shape[0] // ST
    NCOL = routed.shape[0] // P
    NBLK = attn.shape[0] // P
    TOPK = 2
    ROUND = 1.5 * 2 ** 23
    IT = [(lo, min(P, I - lo)) for lo in range(0, I, P)]
    NI = len(IT)
    FULL = I // P

    def sb(name, shape, dt):
        return ctx.enter_context(nc.sbuf_tensor("e_" + name, shape, dt))

    def bank(name, shape):
        return ctx.enter_context(nc.psum_tensor("e_" + name, shape, f32))

    def sem(name):
        return sems.enter_context(nc.semaphore("e_" + name))

    ident = sb("ident", [P, P], f32)
    raw = [sb("raw_g", [P, HT, I], f32), sb("raw_u", [P, HT, I], f32), sb("raw_d", [P, NI, H], f32)]
    hi = [[sb(f"hi_{w}{n}", raw[k].shape, f32r) for k, w in enumerate("gud")] for n in range(2)]
    lo = [[sb(f"lo_{w}{n}", raw[k].shape, f32r) for k, w in enumerate("gud")] for n in range(2)]
    token_of = sb("token_of", [P, NCOL], u32)
    now = sb("now", [P, SB], u32)
    rows = sb("rows", [P, SB, H], f32)
    x_hi, x_lo = sb("x_hi", [P, HT, ST], f32r), sb("x_lo", [P, HT, ST], f32r)
    silu = [sb(f"silu{n}", [P, ST], f32) for n in range(NI)]
    h_f = [sb(f"h_f{n}", [P, ST], f32) for n in range(NI)]
    h_hi = [sb(f"h_hi{n}", [P, ST], f32r) for n in range(NI)]
    h_lo = [sb(f"h_lo{n}", [P, ST], f32r) for n in range(NI)]
    zeros = sb("zeros", [P, SB, H], f32)
    y = sb("y", [P, SB, H], f32)
    before, every = sb("before", [P, P], f32), sb("every", [P, P], f32)
    iota_e, iota_r, iota_c = sb("iota_e", [P, NE], f32), sb("iota_r", [P, P], f32), sb("iota_c", [P, NCOL], f32)
    token = sb("token", [P, NBLK], f32)
    big = {n: sb(n, [P, NBLK, NE], f32) for n in ("shifted", "expd", "prob", "eq", "cand", "rest", "one1", "one2",
                                                   "both", "rank", "count", "scan0", "scan1", "place", "pick")}
    row = {n: sb(n, [P, NBLK], f32) for n in ("mx", "sum", "inv", "m1", "m2", "i1", "i2", "ws", "wi", "sge", "sgd", "pf")}
    small = {n: sb(n, [P, NE], f32) for n in ("total", "tiles", "cs0", "cs1", "cs2", "start")}
    bounds_f = sb("bounds_f", [P, NE + 1], f32)
    slot_row, slot_col = sb("slot_row", [P, TOPK, NBLK], f32), sb("slot_col", [P, TOPK, NBLK], f32)
    RO = 4
    is_row = [sb(f"is_row{n}", [P, P], f32) for n in range(RO)]
    token_at = [sb(f"token_at{n}", [P, NCOL], f32) for n in range(RO)]
    ps_r = bank("ps_r", [P, 2, NBLK, NE])
    ps_id = ps_r[:].rearrange("p a b e -> p (a b e)")[:, 0:NCOL]
    ps_t = [bank(f"ps_t{n}", [P, HT // 2, ST]) for n in range(2)]
    ps_h = [bank(f"ps_h{n}", [P, 2, ST]) for n in range(NI)]
    ps_y = [bank(f"ps_y{n}", [P, H]) for n in range(SB)]

    chain, shifted, expd, both, ranked, copied, bounds_done = (sem(n) for n in (
        "chain", "shifted", "expd", "both", "ranked", "copied", "bounds_done"))
    hot, id_mm, ids_done = sem("hot"), sem("id_mm"), sem("ids_done")
    base, consts, raw_in = sem("base"), sem("consts"), sem("raw_in")
    hi_done, lo_done = sem("hi_done"), sem("lo_done")
    now_done, rows_in = sem("now_done"), sem("rows_in")
    t_mm, h_mm, y_mm = sem("t_mm"), sem("h_mm"), sem("y_mm")
    xhi_done, xlo_done = sem("xhi_done"), sem("xlo_done")
    silu_done, h_done, hhi_done, h_split = sem("silu_done"), sem("h_done"), sem("hhi_done"), sem("h_split")
    y_done, stored = sem("y_done"), sem("stored")
    NPARTS = 4

    def pieces(n):
        for k in range(2):
            yield lambda t, k=k: t[k][:, :, :]
        yield lambda t: t[2][:, 0:FULL, :]
        yield lambda t: t[2][0:I - FULL * P, FULL, :]

    def alone(eng, s, value, met, met_value):
        if not isinstance(value, int):
            value = eng.to_reg(value)
            eng.wait_ge(met, met_value)
        eng.wait_ge(s, value)

    def each_expert(eng, start, tile):
        def one(e, n):
            first = eng.value_load(keep["bounds"][0:1, bass.ds(e, 1)], min_val=0, max_val=NTILES - 2)
            last = eng.value_load(keep["bounds"][0:1, bass.ds(e + 1, 1)], min_val=1, max_val=NTILES - 1)
            start(e, n, first)
            with eng.Fori(first, last) as j:
                tile(j, n)

        with eng.Fori(0, NE // 2 - 1) as pair:
            for n in range(2):
                one(2 * pair + n, n)
        for n in range(2):
            one(NE - 2 + n, n)

    def exists(e):
        return not isinstance(e, int) or e < NE

    block = ctx.enter_context(nc.Block())

    @block.sync
    def _(sp):
        def load(e):
            for k, w in enumerate((w_gate, w_up)):
                sp.dma_start(raw[k][:], w[bass.ds(e, 1), :, :].rearrange("e (k p) i -> p (e k) i", p=P)).then_inc(raw_in, 16)
            sp.dma_start(raw[2][:, 0:FULL, :], w_down[bass.ds(e, 1), 0:FULL * P, :].rearrange("e (k p) h -> p (e k) h", p=P)).then_inc(raw_in, 16)
            sp.dma_start(raw[2][0:I - FULL * P, FULL, :], w_down[bass.ds(e, 1), FULL * P:I, :].rearrange("e p h -> p (e h)")).then_inc(raw_in, 16)

        load(0)
        sp.wait_ge(lo_done, NPARTS)
        load(1)
        sp.wait_ge(bounds_done, 1)

        def start(e, n, first):
            if exists(e + 2):
                sp.wait_ge(lo_done, NPARTS * (e + 2))
                load(e + 2)

        def tile(j, n):
            sp.wait_ge(y_done, SB * (j + 1) + SB)
            sp.dma_start(routed[bass.ds(j * ST, ST), :].rearrange("(s p) h -> p s h", p=P), y[:]).then_inc(stored, 16)

        each_expert(sp, start, tile)
        total = sp.value_load(keep["bounds"][0:1, NE:NE + 1], min_val=1, max_val=NTILES - 1)
        sp.wait_ge(consts, 8)
        with sp.Fori(total, NTILES) as j:
            sp.dma_start(routed[bass.ds(j * ST, ST), :].rearrange("(s p) h -> p s h", p=P), zeros[:]).then_inc(stored, 16)
        sp.wait_ge(stored, 16 * NTILES + 16)

    @block.gpsimd
    def _(pool):
        pool.memset(ident[:], 0.0).then_inc(base, 1)
        pool.memset(before[:], 0.0).then_inc(base, 1)
        pool.iota(iota_e[:], pattern=[[1, NE]], base=0, channel_multiplier=0, allow_small_or_imprecise_dtypes=True).then_inc(consts, 1)
        pool.wait_ge(base, 2)
        pool.affine_select(out=before[:], in_=before[:], compare_op=ALU.is_ge, fill=1.0, base=0,
                           pattern=[[-1, P]], channel_multiplier=1).then_inc(consts, 1)
        pool.memset(every[:], 1.0).then_inc(consts, 1)
        pool.affine_select(out=ident[:], in_=ident[:], compare_op=ALU.not_equal, fill=1.0, base=0,
                           pattern=[[-1, P]], channel_multiplier=1).then_inc(consts, 1)
        for tile, step, across in ((iota_r, 1, 0), (iota_c, 1, 0), (token, P, 1)):
            pool.iota(tile[:], pattern=[[step, tile.shape[1]]], base=0, channel_multiplier=across,
                      allow_small_or_imprecise_dtypes=True).then_inc(consts, 1)
        pool.memset(zeros[:], 0.0).then_inc(consts, 1)
        pool.wait_ge(bounds_done, 1)
        pool.wait_ge(ids_done, 1)

        def gather(j):
            pool.tensor_copy(now[:], token_of[:, bass.ds(j * SB, SB)]).then_inc(now_done, 1)
            alone(pool, now_done, j + 1, ids_done, 1)
            for s in range(SB):
                pool.indirect_dma_start(out=rows[:, s, :], out_offset=None, in_=attn,
                                        in_offset=bass.IndirectOffsetOnAxis(ap=now[:, s:s + 1], axis=0)).then_inc(rows_in, 16)

        gather(0)

        def tile(j, n):
            pool.wait_ge(rows_in, 16 * SB * (j + 1))
            pool.wait_ge(t_mm, 2 * (j + 1))
            gather(j + 1)

        each_expert(pool, lambda e, n, first: None, tile)
        total = pool.value_load(keep["bounds"][0:1, NE:NE + 1], min_val=1, max_val=NTILES - 1)
        pool.wait_ge(rows_in, 16 * SB * (total + 1))

    @block.scalar
    def _(act):
        def split(e, n):
            act.wait_ge(raw_in, 16 * NPARTS * (e + 1))
            for part in pieces(n):
                act.activation(part(hi[n]), part(raw), ACT.Copy).then_inc(hi_done, 1)

        def x_high(j):
            for a in range(2):
                act.wait_ge(t_mm, 2 * j + a + 1)
                act.activation(x_hi[:, a * HT // 2:(a + 1) * HT // 2, :], ps_t[a][:], ACT.Copy).then_inc(xhi_done, 1)

        act.wait_ge(shifted, 1)
        act.activation(big["expd"][:], big["shifted"][:], ACT.Exp).then_inc(expd, 1)
        act.activation(row["sge"][:], keep["logits"][:, :, NE], ACT.Exp, scale=-1.0).then_inc(expd, 1)
        act.sem_inc(y_done, SB)
        act.sem_inc(stored, 16)
        split(0, 0)
        x_high(0)
        act.wait_ge(bounds_done, 1)

        def start(e, n, first):
            if exists(e + 1):
                act.wait_ge(y_mm, SB * first + SB)
                split(e + 1, 1 - n)

        def tile(j, n):
            for t, (_, width) in enumerate(IT):
                act.wait_ge(h_mm, NI * j + t + 1)
                act.wait_ge(h_done, NI * j + t + 1)
                act.activation(silu[t][0:width, :], ps_h[t][0:width, 0, :], ACT.Silu).then_inc(silu_done, 1)
            x_high(j + 1)
            for s in range(SB):
                act.wait_ge(y_mm, SB * j + s + 1 + SB)
                if s == 0:
                    act.wait_ge(stored, 16 * (j + 1))
                act.activation(y[:, s, :], ps_y[s][:], ACT.Copy).then_inc(y_done, 1)

        each_expert(act, start, tile)


    @block.vector
    def _(dve):
        def split(e, n):
            for k, part in enumerate(pieces(n)):
                dve.wait_ge(hi_done, NPARTS * e + k + 1)
                dve.tensor_tensor(part(lo[n]), part(raw), part(hi[n]), ALU.subtract).then_inc(lo_done, 1)

        def x_low(j):
            for a in range(2):
                dve.wait_ge(xhi_done, 2 * j + a + 1)
                ks = slice(a * HT // 2, (a + 1) * HT // 2)
                dve.tensor_tensor(x_lo[:, ks, :], ps_t[a][:], x_hi[:, ks, :], ALU.subtract).then_inc(xlo_done, 1)

        dve.wait_ge(consts, 8)
        done = [0]

        def link(ins):
            done[0] += 1
            ins.then_inc(chain, 1)
            dve.wait_ge(chain, done[0])

        def wide(ap):
            return ap.rearrange("p (b a) -> p b a", a=1).to_broadcast([P, NBLK, NE])

        def narrow(ap):
            return ap.rearrange("p (a e) -> p a e", a=1).to_broadcast([P, NBLK, NE])

        B, R, S = big, row, small
        link(dve.reduce_max(R["mx"][:], keep["logits"][:, :, 0:NE], AX.X))
        dve.tensor_tensor(B["shifted"][:], keep["logits"][:, :, 0:NE], wide(R["mx"][:]), ALU.subtract).then_inc(shifted, 1)
        dve.wait_ge(expd, 2)
        link(dve.reduce_sum(R["sum"][:], B["expd"][:], AX.X))
        link(dve.reciprocal(R["inv"][:], R["sum"][:]))
        link(dve.tensor_tensor(B["prob"][:], B["expd"][:], wide(R["inv"][:]), ALU.mult))
        src = "prob"
        for m, ind, one, k in (("m1", "i1", "one1", 0), ("m2", "i2", "one2", 1)):
            link(dve.reduce_max(R[m][:], B[src][:], AX.X))
            link(dve.tensor_tensor(B["eq"][:], B[src][:], wide(R[m][:]), ALU.is_equal))
            link(dve.tensor_scalar(B["cand"][:], B["eq"][:], -float(NE), None, ALU.mult))
            link(dve.tensor_tensor(B["cand"][:], B["cand"][:], narrow(iota_e[:]), ALU.add))
            link(dve.tensor_reduce(R[ind][:], B["cand"][:], AX.X, ALU.min))
            link(dve.tensor_scalar(R[ind][:], R[ind][:], float(NE), None, ALU.add))
            link(dve.tensor_tensor(B[one][:], narrow(iota_e[:]), wide(R[ind][:]), ALU.is_equal))
            if k == 0:
                link(dve.tensor_scalar(B["cand"][:], B["one1"][:], -2.0, None, ALU.mult))
                link(dve.tensor_tensor(B["rest"][:], B["prob"][:], B["cand"][:], ALU.add))
                src = "rest"
        dve.tensor_tensor(B["both"][:], B["one1"][:], B["one2"][:], ALU.add).then_inc(both, 1)
        link(dve.tensor_tensor(R["ws"][:], R["m1"][:], R["m2"][:], ALU.add))
        link(dve.reciprocal(R["wi"][:], R["ws"][:]))
        link(dve.tensor_tensor(keep["weight"][:, 0, :], R["m1"][:], R["wi"][:], ALU.mult))
        link(dve.tensor_tensor(keep["weight"][:, 1, :], R["m2"][:], R["wi"][:], ALU.mult))
        link(dve.tensor_scalar(R["sgd"][:], R["sge"][:], 1.0, None, ALU.add))
        link(dve.reciprocal(keep["shared_gate"][:], R["sgd"][:]))
        dve.wait_ge(ranked, 2)
        dve.tensor_copy(B["rank"][:], ps_r[:, 0]).then_inc(copied, 1)
        dve.tensor_copy(B["count"][:], ps_r[:, 1]).then_inc(copied, 1)
        dve.wait_ge(copied, 2)
        link(dve.tensor_copy(B["scan0"][:], B["count"][:]))
        a, b, d = "scan0", "scan1", 1
        while d < NBLK:
            link(dve.tensor_copy(B[b][:, 0:d, :], B[a][:, 0:d, :]))
            link(dve.tensor_tensor(B[b][:, d:, :], B[a][:, d:, :], B[a][:, 0:NBLK - d, :], ALU.add))
            a, b, d = b, a, 2 * d
        link(dve.tensor_scalar(S["total"][:], B[a][:, NBLK - 1, :], 1.0 / ST, (ST - 1.0) / ST - 0.5 + 0.25 / ST, ALU.mult, ALU.add))
        link(dve.tensor_scalar(S["tiles"][:], S["total"][:], ROUND, -ROUND, ALU.add, ALU.add))
        link(dve.tensor_scalar(S["tiles"][:], S["tiles"][:], 1.0, None, ALU.max))
        c, e, d = "tiles", "cs0", 1
        while d < NE:
            link(dve.tensor_copy(S[e][:, 0:d], S[c][:, 0:d]))
            link(dve.tensor_tensor(S[e][:, d:], S[c][:, d:], S[c][:, 0:NE - d], ALU.add))
            c, e, d = e, {"cs0": "cs1", "cs1": "cs2"}.get(e), 2 * d
        link(dve.memset(bounds_f[:, 0:1], 0.0))
        link(dve.tensor_copy(bounds_f[:, 1:], S[c][:]))
        dve.tensor_copy(keep["bounds"][:], bounds_f[:]).then_inc(bounds_done, 1)
        link(dve.tensor_scalar(S["start"][:], bounds_f[:, 0:NE], float(ST), None, ALU.mult))
        link(dve.tensor_tensor(B["place"][:], B[a][:], B["count"][:], ALU.subtract))
        link(dve.tensor_tensor(B["place"][:], B["place"][:], B["rank"][:], ALU.add))
        link(dve.tensor_tensor(B["place"][:], B["place"][:], narrow(S["start"][:]), ALU.add))
        for k, one in enumerate(("one1", "one2")):
            link(dve.tensor_tensor(B["pick"][:], B["place"][:], B[one][:], ALU.mult))
            link(dve.reduce_sum(R["pf"][:], B["pick"][:], AX.X))
            link(dve.tensor_copy(keep["slot"][:, k, :], R["pf"][:]))
            link(dve.tensor_scalar(slot_col[:, k, :], R["pf"][:], 1.0 / P, -0.5 + 0.5 / P, ALU.mult, ALU.add))
            link(dve.tensor_scalar(slot_col[:, k, :], slot_col[:, k, :], ROUND, -ROUND, ALU.add, ALU.add))
            link(dve.tensor_scalar(slot_row[:, k, :], slot_col[:, k, :], -float(P), None, ALU.mult))
            link(dve.tensor_tensor(slot_row[:, k, :], slot_row[:, k, :], R["pf"][:], ALU.add))

        def hot_ones(i, n):
            k, b = n % 2, bass.ds(2 * i + n // 2, 1)
            m = RO * i + n
            if not isinstance(i, int) or i:
                dve.wait_ge(id_mm, m - RO + 1)
            dve.tensor_scalar(is_row[n][:], iota_r[:], slot_row[:, k, b], None, ALU.is_equal).then_inc(hot, 1)
            dve.tensor_scalar(token_at[n][:], iota_c[:], slot_col[:, k, b], token[:, b], ALU.is_equal, ALU.mult).then_inc(hot, 1)

        for n in range(RO):
            hot_ones(0, n)
        with dve.Fori(1, TOPK * NBLK // RO) as i:
            for n in range(RO):
                hot_ones(i, n)
        dve.wait_ge(id_mm, TOPK * NBLK)
        dve.tensor_copy(token_of[:], ps_id).then_inc(ids_done, 1)

        dve.sem_inc(h_done, NI)
        split(0, 0)
        x_low(0)

        def start(e, n, first):
            if exists(e + 1):
                split(e + 1, 1 - n)

        def tile(j, n):
            for t, (_, width) in enumerate(IT):
                w = slice(0, width)
                dve.wait_ge(silu_done, NI * j + t + 1)
                dve.tensor_tensor(h_f[t][w, :], silu[t][w, :], ps_h[t][w, 1, :], ALU.mult).then_inc(h_done, 1)
                dve.wait_ge(h_done, NI * j + t + 1 + NI)
                dve.tensor_copy(h_hi[t][w, :], h_f[t][w, :]).then_inc(hhi_done, 1)
                dve.wait_ge(hhi_done, NI * j + t + 1)
                dve.tensor_tensor(h_lo[t][w, :], h_f[t][w, :], h_hi[t][w, :], ALU.subtract).then_inc(h_split, 1)
            x_low(j + 1)

        each_expert(dve, start, tile)

    @block.tensor
    def _(pe):
        pe.wait_ge(consts, 8)
        pe.wait_ge(both, 1)
        pairs = big["both"][:].rearrange("p b e -> p (b e)")
        for k, left in enumerate((before, every)):
            nc.tensor.matmul(ps_r[:, k].rearrange("p b e -> p (b e)"), left[:], pairs, start=True, stop=True).then_inc(ranked, 1)

        def place_tokens(i, n):
            m = RO * i + n
            pe.wait_ge(hot, 2 * (m + 1))
            last = isinstance(i, int) and i > 0 and n == RO - 1
            nc.tensor.matmul(ps_id, is_row[n][:], token_at[n][:], start=(isinstance(i, int) and m == 0), stop=last).then_inc(id_mm, 1)

        pe.wait_ge(copied, 2)
        for n in range(RO):
            place_tokens(0, n)
        with pe.Fori(1, TOPK * NBLK // RO - 1) as i:
            for n in range(RO):
                place_tokens(i, n)
        for n in range(RO):
            place_tokens(TOPK * NBLK // RO - 1, n)
        pe.wait_ge(bounds_done, 1)
        pe.sem_inc(y_mm, SB)

        def turn(j):
            pe.wait_ge(rows_in, 16 * SB * (j + 1))
            for a in range(2):
                for m in range(HT // 2):
                    k = a * HT // 2 + m
                    for s in range(SB):
                        last = nc.tensor.transpose(ps_t[a][:, m, s * P:(s + 1) * P], rows[:, s, k * P:(k + 1) * P], ident[:])
                last.then_inc(t_mm, 1)

        turn(0)

        def start(e, n, first):
            alone(pe, lo_done, NPARTS * (e + 1), consts, 8)

        def tile(j, n):
            pe.wait_ge(xlo_done, 2 * (j + 1))
            for t, (at, width) in enumerate(IT):
                pe.wait_ge(h_done, NI * j + t + 1)
                for k in range(2):
                    terms = [(m, l, r) for m in range(HT) for l, r in ((hi[n], x_hi), (hi[n], x_lo), (lo[n], x_hi))]
                    for c, (m, l, r) in enumerate(terms):
                        last = nc.tensor.matmul(ps_h[t][0:width, k, :], l[k][:, m, at:at + width], r[:, m, :],
                                                start=(c == 0), stop=(c == len(terms) - 1))
                last.then_inc(h_mm, 1)
            turn(j + 1)
            for t, (_, width) in enumerate(IT):
                pe.wait_ge(h_split, NI * j + t + 1)
                w = slice(0, width)
                for s in range(SB):
                    if t == 0:
                        pe.wait_ge(y_done, SB * j + s + 1)
                    c = slice(s * P, (s + 1) * P)
                    for m, (l, r) in enumerate(((h_hi, hi[n]), (h_hi, lo[n]), (h_lo, hi[n]))):
                        last = nc.tensor.matmul(ps_y[s][:], l[t][w, c], r[2][w, t, :],
                                                start=(t == 0 and m == 0), stop=(t == NI - 1 and m == 2))
                    if t == NI - 1:
                        last.then_inc(y_mm, 1)

        each_expert(pe, start, tile)


def shared(nc, ctx, sems, keep, x, attn, sw_gate, sw_up, sw_down, routed, out):
    import concourse.bass as bass
    from concourse import mybir

    f32, f32r, u32 = mybir.dt.float32, mybir.dt.float32r, mybir.dt.uint32
    ALU, ACT = mybir.AluOpType, mybir.ActivationFunctionType
    P = 128
    NTOK, H = attn.shape
    I = sw_gate.shape[1]
    HT, NI = H // P, I // P
    GT = 512
    GB = GT // P
    NG = NTOK // GT
    TOPK = 2

    def sb(name, shape, dt):
        return ctx.enter_context(nc.sbuf_tensor("s_" + name, shape, dt))

    def bank(name):
        return ctx.enter_context(nc.psum_tensor("s_" + name, [P, 512], f32))

    def sem(name):
        return sems.enter_context(nc.semaphore("s_" + name))

    ident = sb("ident", [P, P], f32)
    raw_gu = [sb(f"raw_gu{n}", [P, 2, HT, P], f32) for n in range(2)]
    raw_d = [sb(f"raw_d{n}", [P, H], f32) for n in range(2)]
    gu_hi, gu_lo = sb("gu_hi", [P, NI, 2, HT, P], f32r), sb("gu_lo", [P, NI, 2, HT, P], f32r)
    d_hi, d_lo = sb("d_hi", [P, NI, H], f32r), sb("d_lo", [P, NI, H], f32r)
    rows = sb("rows", [P, GB, H], f32)
    x_hi, x_lo = sb("x_hi", [P, HT, GT], f32r), sb("x_lo", [P, HT, GT], f32r)
    silu, h_f = sb("silu", [P, GT], f32), sb("h_f", [P, GT], f32)
    h_hi, h_lo = ([sb(f"h_{w}{n}", [P, GT], f32r) for n in range(2)] for w in ("hi", "lo"))
    slot_now, scale_now = sb("slot_now", [P, TOPK, GB], u32), sb("scale_now", [P, TOPK + 1, GB], f32)
    chosen = [[sb(f"chosen{k}{n}", [P, H], f32) for n in range(2)] for k in range(TOPK)]
    total = [sb(f"total{n}", [P, H], f32) for n in range(GB)]
    ps_t = [bank(f"ps_t{n}") for n in range(2)]
    ps_g, ps_u = bank("ps_g"), bank("ps_u")
    ps_y = [bank(f"ps_y{n}") for n in range(GB)]

    base, consts = sem("base"), sem("consts")
    raw_in = [sem(f"raw_in{n}") for n in range(2)]
    w_hi, w_lo = sem("w_hi"), sem("w_lo")
    rows_in, residual_in, stored = sem("rows_in"), [sem(f"residual_in{n}") for n in range(GB)], [sem(f"stored{n}") for n in range(GB)]
    chosen_in = [sem(f"chosen_in{n}") for n in range(2)]
    t_mm, g_mm, u_mm, y_mm = sem("t_mm"), sem("g_mm"), sem("u_mm"), sem("y_mm")
    xhi_done, xlo_done = sem("xhi_done"), sem("xlo_done")
    silu_done, h_done, hhi_done, h_split = sem("silu_done"), sem("h_done"), sem("hhi_done"), sem("h_split")
    slot_done, scale_done, y_read, sum_done, out_ready = sem("slot_done"), sem("scale_done"), sem("y_read"), sem("sum_done"), sem("out_ready")

    x_v = x.rearrange("b d t -> (b d) t")
    out_v = out.rearrange("b d t -> (b d) t")

    def upto(eng, s, value):
        if not (isinstance(value, int) and value <= 0):
            eng.wait_ge(s, value)

    def alone(eng, s, value, met, met_value):
        if not isinstance(value, int):
            value = eng.to_reg(value)
            eng.wait_ge(met, met_value)
        eng.wait_ge(s, value)

    def groups(eng, group):
        group(0)
        with eng.Fori(1, NG - 1) as g:
            group(g)
        group(NG - 1)

    def more(g):
        return not isinstance(g, int) or g + 1 < NG

    block = ctx.enter_context(nc.Block())

    @block.sync
    def _(sp):
        def load_rows(g):
            sp.dma_start(rows[:], attn[bass.ds(g * GT, GT), :].rearrange("(s p) h -> p s h", p=P)).then_inc(rows_in, 16)

        load_rows(0)
        for t in range(NI):
            c = slice(t * P, (t + 1) * P)
            upto(sp, w_lo, 2 * (t - 1))
            for k, w in enumerate((sw_gate, sw_up)):
                sp.dma_start(raw_gu[t % 2][:, k, :, :], w[:, c].rearrange("(k p) i -> p k i", p=P)).then_inc(raw_in[t % 2], 16)
            sp.dma_start(raw_d[t % 2][:], sw_down[c, :]).then_inc(raw_in[t % 2], 16)

        def group(g):
            if more(g):
                sp.wait_ge(t_mm, HT * (g + 1))
                load_rows(g + 1)
            if not isinstance(g, int) or g:
                store(g - 1)
            for s in range(GB):
                upto(sp, stored[s], 16 * g)
                sp.dma_start(total[s][:], x_v[bass.ds((GB * g + s) * P, P), :]).then_inc(residual_in[s], 16)

        def store(g):
            for s in range(GB):
                b = GB * g + s
                sp.wait_ge(out_ready, b + 1)
                sp.dma_start(out_v[bass.ds(b * P, P), :], total[s][:]).then_inc(stored[s], 16)

        groups(sp, group)
        store(NG - 1)
        for s in range(GB):
            sp.wait_ge(stored[s], 16 * NG)

    @block.gpsimd
    def _(pool):
        pool.memset(ident[:], 0.0).then_inc(base, 1)
        pool.wait_ge(base, 1)
        pool.affine_select(out=ident[:], in_=ident[:], compare_op=ALU.not_equal, fill=1.0, base=0,
                           pattern=[[-1, P]], channel_multiplier=1).then_inc(consts, 1)

        def group(g):
            for n in range(2):
                upto(pool, chosen_in[n], 16 * TOPK * 2 * g)
            pool.tensor_copy(slot_now[:], keep["slot"][:, :, bass.ds(GB * g, GB)]).then_inc(slot_done, 1)
            pool.wait_ge(slot_done, g + 1)
            for s in range(GB):
                b = GB * g + s
                if not (isinstance(b, int) and b <= 1):
                    alone(pool, out_ready, b - 1, consts, 1)
                for k in range(TOPK):
                    pool.indirect_dma_start(out=chosen[k][s % 2][:], out_offset=None, in_=routed,
                                            in_offset=bass.IndirectOffsetOnAxis(ap=slot_now[:, k, s:s + 1], axis=0)).then_inc(chosen_in[s % 2], 16)

        groups(pool, group)

    @block.scalar
    def _(act):
        def x_high(g):
            for m in range(HT):
                act.wait_ge(t_mm, HT * g + m + 1)
                act.activation(x_hi[:, m, :], ps_t[m % 2][:], ACT.Copy).then_inc(xhi_done, 1)

        def split(t):
            act.wait_ge(raw_in[t % 2], 16 * 3 * (t // 2 + 1))
            act.activation(gu_hi[:, t], raw_gu[t % 2][:], ACT.Copy).then_inc(w_hi, 1)
            act.activation(d_hi[:, t], raw_d[t % 2][:], ACT.Copy).then_inc(w_hi, 1)

        def group(g):
            first = isinstance(g, int) and g == 0
            for t in range(NI):
                if first and t + 2 < NI:
                    split(t + 2)
                act.wait_ge(g_mm, NI * g + t + 1)
                upto(act, h_done, NI * g + t)
                act.activation(silu[:], ps_g[:], ACT.Silu).then_inc(silu_done, 1)
            if more(g):
                act.wait_ge(u_mm, NI * (g + 1))
                x_high(g + 1)

        x_high(0)
        split(0)
        split(1)
        groups(act, group)

    @block.vector
    def _(dve):
        def x_low(g):
            for m in range(HT):
                dve.wait_ge(xhi_done, HT * g + m + 1)
                dve.tensor_tensor(x_lo[:, m, :], ps_t[m % 2][:], x_hi[:, m, :], ALU.subtract).then_inc(xlo_done, 1)

        def split(t):
            dve.wait_ge(w_hi, 2 * t + 1)
            dve.tensor_tensor(gu_lo[:, t], raw_gu[t % 2][:], gu_hi[:, t], ALU.subtract).then_inc(w_lo, 1)
            dve.wait_ge(w_hi, 2 * t + 2)
            dve.tensor_tensor(d_lo[:, t], raw_d[t % 2][:], d_hi[:, t], ALU.subtract).then_inc(w_lo, 1)

        def group(g):
            first = isinstance(g, int) and g == 0
            for t in range(NI):
                if first and t + 2 < NI:
                    split(t + 2)
                n = NI * g + t
                dve.wait_ge(silu_done, n + 1)
                dve.wait_ge(u_mm, n + 1)
                upto(dve, h_split, n)
                dve.tensor_tensor(h_f[:], silu[:], ps_u[:], ALU.mult).then_inc(h_done, 1)
                dve.wait_ge(h_done, n + 1)
                upto(dve, y_mm, n if t == 0 else n - 1)
                dve.tensor_copy(h_hi[t % 2][:], h_f[:]).then_inc(hhi_done, 1)
                dve.wait_ge(hhi_done, n + 1)
                dve.tensor_tensor(h_lo[t % 2][:], h_f[:], h_hi[t % 2][:], ALU.subtract).then_inc(h_split, 1)
                if t < GB and (not isinstance(g, int) or g):
                    add_chosen(g - 1, t)
            if more(g):
                x_low(g + 1)
            upto(dve, out_ready, GB * g)
            dve.tensor_copy(scale_now[:, 0:TOPK, :], keep["weight"][:, :, bass.ds(GB * g, GB)]).then_inc(scale_done, 1)
            dve.tensor_copy(scale_now[:, TOPK, :], keep["shared_gate"][:, bass.ds(GB * g, GB)]).then_inc(scale_done, 1)
            dve.wait_ge(scale_done, 2 * (g + 1))
            dve.wait_ge(y_mm, NI * (g + 1))
            for s in range(GB):
                dve.wait_ge(residual_in[s], 16 * (g + 1))
                dve.scalar_tensor_tensor(out=total[s][:], in0=ps_y[s][:], scalar=scale_now[:, TOPK, s:s + 1],
                                         in1=total[s][:], op0=ALU.mult, op1=ALU.add).then_inc(y_read, 1)

        def add_chosen(g, s):
            b = GB * g + s
            dve.wait_ge(chosen_in[s % 2], 16 * TOPK * (2 * g + s // 2 + 1))
            dve.wait_ge(y_read, b + 1)
            dve.scalar_tensor_tensor(out=total[s][:], in0=chosen[0][s % 2][:], scalar=scale_now[:, 0, s:s + 1],
                                     in1=total[s][:], op0=ALU.mult, op1=ALU.add).then_inc(sum_done, 1)
            dve.wait_ge(sum_done, b + 1)
            dve.scalar_tensor_tensor(out=total[s][:], in0=chosen[1][s % 2][:], scalar=scale_now[:, 1, s:s + 1],
                                     in1=total[s][:], op0=ALU.mult, op1=ALU.add).then_inc(out_ready, 1)

        x_low(0)
        split(0)
        split(1)
        groups(dve, group)
        for s in range(GB):
            add_chosen(NG - 1, s)

    @block.tensor
    def _(pe):
        pe.wait_ge(consts, 1)

        def turn(g, m):
            if m == 0:
                pe.wait_ge(rows_in, 16 * (g + 1))
            upto(pe, xlo_done, HT * g + m - 1)
            for s in range(GB):
                last = nc.tensor.transpose(ps_t[m % 2][:, s * P:(s + 1) * P], rows[:, s, m * P:(m + 1) * P], ident[:])
            last.then_inc(t_mm, 1)

        def up(g, t, k, ps, s, mm):
            terms = [(m, l, r) for m in range(HT) for l, r in ((gu_hi, x_hi), (gu_hi, x_lo), (gu_lo, x_hi))]
            for c, (m, l, r) in enumerate(terms):
                last = nc.tensor.matmul(ps[:], l[:, t, k, m, :], r[:, m, :], start=(c == 0), stop=(c == len(terms) - 1))
            last.then_inc(mm, 1)

        def down(g, t):
            n = NI * g + t
            pe.wait_ge(h_split, n + 1)
            for s in range(GB):
                if t == 0:
                    upto(pe, y_read, GB * g - GB + s + 1 if not isinstance(g, int) or g else 0)
                c = slice(s * P, (s + 1) * P)
                for m, (l, r) in enumerate(((h_hi, d_hi), (h_hi, d_lo), (h_lo, d_hi))):
                    last = nc.tensor.matmul(ps_y[s][:], l[t % 2][:, c], r[:, t, :], start=(t == 0 and m == 0), stop=(t == NI - 1 and m == 2))
            last.then_inc(y_mm, 1)

        def group(g):
            first = isinstance(g, int) and g == 0
            for t in range(NI):
                n = NI * g + t
                if t == 0:
                    pe.wait_ge(xlo_done, HT * (g + 1))
                if first:
                    pe.wait_ge(w_lo, 2 * (t + 1))
                if t == NI - 1 and more(g):
                    turn(g + 1, 0)
                    turn(g + 1, 1)
                upto(pe, silu_done, n)
                up(g, t, 0, ps_g, silu_done, g_mm)
                upto(pe, h_done, n)
                up(g, t, 1, ps_u, h_done, u_mm)
                if t:
                    down(g, t - 1)
            if more(g):
                turn(g + 1, 2)
                turn(g + 1, 3)
            down(g, NI - 1)

        for m in range(HT):
            turn(0, m)
        groups(pe, group)


def build(nc, x, mask, wq_t, wo_t, gates, w_gate, w_up, w_down, sw_gate, sw_up, sw_down, out):
    from contextlib import ExitStack
    from concourse import mybir

    f32, i32, u32 = mybir.dt.float32, mybir.dt.int32, mybir.dt.uint32
    P = 128
    NB, D, T = x.shape
    NTOK, NE, TOPK = NB * D, w_gate.shape[0], 2
    SLOT_TILE = 256
    NTILES = NTOK * TOPK // SLOT_TILE + NE + 1
    attn = nc.dram_tensor("attn", (NTOK, T), f32, kind="Internal").ap()
    routed = nc.dram_tensor("routed", (NTILES * SLOT_TILE, T), f32, kind="Internal").ap()

    with ExitStack() as whole:
        def sb(name, shape, dt):
            return whole.enter_context(nc.sbuf_tensor("keep_" + name, shape, dt))

        keep = {
            "slot": sb("slot", [P, TOPK, NTOK // P], u32),
            "logits": sb("logits", [P, NTOK // P, NE + 1], f32),
            "weight": sb("weight", [P, TOPK, NTOK // P], f32),
            "shared_gate": sb("shared_gate", [P, NTOK // P], f32),
            "bounds": sb("bounds", [P, NE + 1], i32),
            "slot_tile": SLOT_TILE,
        }
        with ExitStack() as ctx:
            attention(nc, ctx, whole, keep, x, mask, wq_t, wo_t, gates, attn)
        with ExitStack() as ctx:
            experts(nc, ctx, whole, keep, attn, w_gate, w_up, w_down, routed)
        with ExitStack() as ctx:
            shared(nc, ctx, whole, keep, x, attn, sw_gate, sw_up, sw_down, routed, out)


def kernel(x, cond_2048, L0_cond_Wq, L0_cond_Wo, L0_ffn_gate_w, L0_ffn_w_gate, L0_ffn_w_up, L0_ffn_w_down,
           L0_ffn_sw_gate, L0_ffn_sw_up, L0_ffn_sw_down, L0_ffn_shared_gate_w):
    import numpy as np
    import concourse.bacc as bacc
    from concourse import mybir
    from concourse.bass_utils import run_bass_kernel_spmd

    D = L0_cond_Wq.shape[0]
    NH, P = 8, 128
    DK = D // NH
    wq_t = np.asarray(L0_cond_Wq).T.reshape(D, D // P, P // DK, DK).transpose(0, 1, 3, 2).reshape(D, D)
    gates = np.concatenate([np.asarray(L0_ffn_gate_w).T, np.asarray(L0_ffn_shared_gate_w)], axis=1)
    arrays = {
        "x": x, "mask": cond_2048, "wq_t": wq_t, "wo_t": np.asarray(L0_cond_Wo).T, "gates": gates,
        "w_gate": L0_ffn_w_gate, "w_up": L0_ffn_w_up, "w_down": L0_ffn_w_down,
        "sw_gate": L0_ffn_sw_gate, "sw_up": L0_ffn_sw_up, "sw_down": L0_ffn_sw_down,
    }
    arrays = {"in_" + n: np.ascontiguousarray(a) for n, a in arrays.items()}
    nc = bacc.Bacc("TRN2", target_bir_lowering=False, num_devices=1)
    args = [nc.dram_tensor(n, a.shape, mybir.dt.from_np(a.dtype), kind="ExternalInput").ap() for n, a in arrays.items()]
    out = nc.dram_tensor("out", x.shape, mybir.dt.float32, kind="ExternalOutput").ap()
    build(nc, *args, out)
    return run_bass_kernel_spmd(nc, [arrays], core_ids=[0]).results[0]["out"]
```

```python
def attention(nc, ctx, sems, keep, x, mask, wqT, woT, gates, attn):
    import concourse.bass as bass
    from concourse import mybir

    f32, f32r = mybir.dt.float32, mybir.dt.float32r
    ALU, ACT, AX = mybir.AluOpType, mybir.ActivationFunctionType, mybir.AxisListType

    NB, D, T = x.shape
    P = 128
    NH = 8
    DK = D // NH
    HG = P // DK
    UPB = NH // HG
    NU = NB * UPB
    KT = D // P
    KB = T // P
    SCALE = float(DK) ** -0.5
    NEG = -1e30
    MASKROW = 3 * DK
    MAXROW = MASKROW + 1
    STK = MAXROW + 1
    RING = 4
    STACK_DMAS = 8
    PARTS = 4

    def sb(name, shape, dt):
        return ctx.enter_context(nc.sbuf_tensor(name, shape, dt))

    def bank(name):
        return ctx.enter_context(nc.psum_tensor(name, [P, 512], f32))

    def sem(name):
        return sems.enter_context(nc.semaphore(name))

    wq_hi, wq_lo = sb("wq_hi", [P, KT, D], f32r), sb("wq_lo", [P, KT, D], f32r)
    wo_hi, wo_lo = sb("wo_hi", [P, KT, D], f32r), sb("wo_lo", [P, KT, D], f32r)
    ident = sb("ident", [P, P], f32)
    ones = sb("ones", [P, DK], f32)
    one_row = sb("one_row", [1, T], f32r)
    NE = gates.shape[1]
    gate_w = sb("gate_w", [P, KB, P // KB], f32)
    xo_t = sb("xo_t", [P, KB, KT * P], f32)
    partial, add_up = sb("partial", [P, KT * P], f32), sb("add_up", [P, NE], f32)
    x_f = [sb(f"x_f{n}", [P, KT, T], f32) for n in range(2)]
    x_hi, x_lo = sb("x_hi", [P, KT, T], f32r), sb("x_lo", [P, KT, T], f32r)
    mask_b = [sb(f"mask_b{n}", [P, T], f32) for n in range(2)]
    row_mask = [sb(f"row_mask{n}", [1, T], f32r) for n in range(2)]
    row_neg = [sb(f"row_neg{n}", [1, T], f32r) for n in range(2)]
    q_f = [sb(f"q_f{n}", [P, T], f32) for n in range(2)]
    q_hi = [sb(f"q_hi{n}", [P, T], f32r) for n in range(2)]
    q_lo = [sb(f"q_lo{n}", [P, T], f32r) for n in range(2)]
    qm_hi = [sb(f"qm_hi{n}", [P, T], f32r) for n in range(2)]
    qm_lo = [sb(f"qm_lo{n}", [P, T], f32r) for n in range(2)]
    kside = [sb(f"kside{n}", [STK, HG, T], f32r) for n in range(RING)]
    qside = [sb(f"qside{n}", [STK, HG, T], f32r) for n in range(RING)]
    v = [sb(f"v{n}", [P, KB, HG, DK], f32) for n in range(RING)]
    maxcol = [sb(f"maxcol{n}", [P, HG * KB], f32) for n in range(2)]
    maxrow = [sb(f"maxrow{n}", [HG * KB, P], f32r) for n in range(2)]
    e = [sb(f"e{n}", [P, HG, T], f32) for n in range(KB)]
    num = [sb(f"num{n}", [P, T], f32) for n in range(2)]
    den = [sb(f"den{n}", [P, T], f32) for n in range(2)]
    wq_f, wo_f = num[0][:].rearrange("p (k d) -> p k d", k=KT), den[0][:].rearrange("p (k d) -> p k d", k=KT)
    c_f = [sb(f"c_f{n}", [P, T], f32) for n in range(2)]
    c_hi = [sb(f"c_hi{n}", [P, T], f32r) for n in range(2 * UPB)]
    c_lo = [sb(f"c_lo{n}", [P, T], f32r) for n in range(2 * UPB)]
    xo = [sb(f"xo{n}", [P, T], f32) for n in range(2)]

    ps_e = [bank(f"ps_e{n}") for n in range(2)]
    ps_m = [bank(f"ps_m{n}") for n in range(2)]
    ps_num, ps_den = bank("ps_num"), bank("ps_den")
    ps_q, ps_o = bank("ps_q"), bank("ps_o")

    one_f = sb("one_f", [1, T], f32)
    w_in = sem("w_in")
    add_up_done, partial_mm, partial_done = sem("add_up_done"), sem("partial_mm"), sem("partial_done")
    gate_in, xt_mm, xt_done, lg_mm, lg_done = (sem(n) for n in ("gate_in", "xt_mm", "xt_done", "lg_mm", "lg_done"))
    zeroed = sem("zeroed")
    ql_done, dve_set = sem("ql_done"), sem("dve_set")
    setup = sem("setup")
    ones_in = sem("ones_in")
    w_split = sem("w_split")
    x_in = [sem(f"x_in{n}") for n in range(2)]
    mask_in = [sem(f"mask_in{n}") for n in range(2)]
    stack_in = [sem(f"stack_in{n}") for n in range(RING)]
    maxrow_in = [sem(f"maxrow_in{n}") for n in range(RING)]
    stored = [sem(f"stored{n}") for n in range(2)]
    e_mm, m_mm, num_mm, den_mm = sem("e_mm"), sem("m_mm"), sem("num_mm"), sem("den_mm")
    pair_dve, pair_pool = sem("pair_dve"), sem("pair_pool")
    q_mm, v_mm, mt_mm, o_mm = sem("q_mm"), sem("v_mm"), sem("mt_mm"), sem("o_mm")
    e_done, q_done, v_done, mt_done = sem("e_done"), sem("q_done"), sem("v_done"), sem("mt_done")
    num_done, den_done, chi_done, o_done = sem("num_done"), sem("den_done"), sem("chi_done"), sem("o_done")
    max_done, c_done, rd_done, rows_done = sem("max_done"), sem("c_done"), sem("rd_done"), sem("rows_done")
    xhi_done, x_split, q_split, c_split = sem("xhi_done"), sem("x_split"), sem("q_split"), sem("c_split")

    def words(ap):
        return ap.bitcast(f32)

    def upto(eng, s, value):
        if not (isinstance(value, int) and value <= 0):
            eng.wait_ge(s, value)

    def alone(eng, s, value, met, met_value):
        if not isinstance(value, int):
            value = eng.to_reg(value)
            eng.wait_ge(met, met_value)
        eng.wait_ge(s, value)

    LOOP_UNITS = RING
    NI = NU // LOOP_UNITS

    def run_units(eng, step, before, after):
        for n in range(before, 0):
            step(-1, RING + n)
        for n in range(LOOP_UNITS):
            step(0, n)
        if NI > 3:
            with eng.Fori(1, NI - 2) as i:
                for n in range(LOOP_UNITS):
                    step(i, n)
        for i in range(max(NI - 2, 1), NI):
            for n in range(LOOP_UNITS):
                step(i, n)
        for n in range(after):
            step(NI, n)

    def known(i, n, off=0, lo=0, hi=NU):
        if isinstance(i, int):
            return lo <= RING * i + n + off < hi
        return True

    def add_pair(eng, u, pair, heads, done):
        k = 2 * pair
        eng.wait_ge(e_done, (KB * u + k + 2) * HG)
        eng.wait_ge(num_mm, KB * u + k + 1)
        into = e[k][:, heads, :]
        eng.tensor_tensor(into, into, e[k + 1][:, heads, :], ALU.add).then_inc(done, 1)

    block = ctx.enter_context(nc.Block())

    @block.sync
    def _(sp):

        def load_x(b, par):
            upto(sp, q_split, UPB * (b - 1))
            upto(sp, rows_done, 2 * (b - 1))
            upto(sp, x_split, b - 1)
            sp.dma_start(x_f[par][:], x[bass.ds(b, 1), :, :].rearrange("b (k p) t -> p (b k) t", p=P)).then_inc(x_in[par], 16)
            sp.dma_start(mask_b[par][:], mask[bass.ds(b, 1), :].to_broadcast([P, T])).then_inc(mask_in[par], 16)

        load_x(0, 0)
        sp.dma_start(wq_f, wqT.rearrange("(k p) c -> p k c", p=P)).then_inc(w_in, 16)
        sp.dma_start(wo_f, woT.rearrange("(k p) c -> p k c", p=P)).then_inc(w_in, 16)
        load_x(1, 1)
        sp.wait_ge(zeroed, 3)
        sp.dma_start(gate_w[:, :, 0:NE], gates.rearrange("(k p) e -> p k e", p=P)).then_inc(gate_in, 16)
        sp.wait_ge(setup, 3)
        for n in range(RING):
            sp.dma_start(words(kside[n][MAXROW:STK, :, :]), words(one_row[0:1, :]).rearrange("p (a t) -> p a t", a=1).to_broadcast([1, HG, T])).then_inc(ones_in, 16)

        def step(i, n):
            u = RING * i + n
            if known(i, n, 3):
                w, slot, par = u + 3, (n + 3) % RING, (n + 3) % 2
                b = 2 * i + (n + 3) // 2
                bp = (n + 3) // 2 % 2
                alone(sp, q_split, w + 1, w_in, 32)
                upto(sp, rows_done, 2 * (b + 1))
                upto(sp, e_mm, (w - RING + 1) * KB * HG)
                for k, (dst, src) in enumerate(((kside, q_hi), (kside, q_hi), (kside, q_lo),
                                                (qside, qm_hi), (qside, qm_lo), (qside, qm_hi))):
                    k = k % 3
                    sp.dma_start(words(dst[slot][k * DK:(k + 1) * DK, :, :]), words(src[par][:, :])).then_inc(stack_in[slot], 16)
                for dst, src in ((kside, row_neg), (qside, row_mask)):
                    sp.dma_start(words(dst[slot][MASKROW:MAXROW, :, :]),
                                 words(src[bp][0:1, :]).rearrange("p (a t) -> p a t", a=1).to_broadcast([1, HG, T])).then_inc(stack_in[slot], 16)
            if known(i, n, 1):
                w, slot, par = u + 1, (n + 1) % RING, (n + 1) % 2
                upto(sp, mt_done, w + 1)
                upto(sp, e_mm, (w - RING + 1) * KB * HG)
                sp.dma_start(words(qside[slot][MAXROW:STK, :, :]), words(maxrow[par][:, :])).then_inc(maxrow_in[slot], 16)
            if n % 2 == 1:
                if known(i, n, 7):
                    load_x(2 * i + (n + 7) // 2, (n + 7) // 2 % 2)
                if known(i, n, -3, hi=NU):
                    for half in range(KT):
                        b = 2 * i + (n - 3) // 2
                        upto(sp, o_done, KT * b + half + 1)
                        sp.dma_start(attn[bass.ds(b * D + half * P, P), :], xo[half][:, :]).then_inc(stored[half], 16)

        run_units(sp, step, -4, 4)
        for half in range(KT):
            sp.wait_ge(stored[half], 16 * NB)

    @block.gpsimd
    def _(pool):
        for tile in (ident, gate_w, add_up):
            pool.memset(tile[:], 0.0).then_inc(zeroed, 1)
        pool.memset(ones[:], 1.0).then_inc(setup, 1)
        pool.wait_ge(zeroed, 3)
        pool.affine_select(out=ident[:], in_=ident[:], compare_op=ALU.not_equal, fill=1.0, base=0,
                           pattern=[[-1, P]], channel_multiplier=1).then_inc(setup, 1)
        for k in range(KB):
            pool.affine_select(out=add_up[:], in_=add_up[:], compare_op=ALU.not_equal, fill=1.0, base=-k * P // KB,
                               pattern=[[-1, NE]], channel_multiplier=1).then_inc(add_up_done, 1)
            pool.wait_ge(add_up_done, k + 1)

        def step(i, n):
            u = RING * i + n
            if known(i, n, -1):
                add_pair(pool, u - 1, 1, slice(HG // 2, HG), pair_pool)
            if known(i, n, -2):
                w, slot = u - 2, (n - 2) % RING
                upto(pool, chi_done, w + 1)
                pool.tensor_tensor(c_lo[slot][:], c_f[n % 2][:], c_hi[slot][:], ALU.subtract).then_inc(c_split, 1)
            if known(i, n):
                add_pair(pool, u, 0, slice(0, HG), pair_pool)
            if known(i, n, 4):
                w, par, bp = u + 4, n % 2, n // 2
                upto(pool, q_done, 2 * (w + 1))
                pool.wait_ge(mask_in[bp], 16 * (i + 2))
                if known(i, n, 2):
                    upto(pool, stack_in[(n + 2) % RING], 16 * STACK_DMAS * (i + 1 + (n + 2) // RING))
                pool.tensor_tensor(q_lo[par][:], q_f[par][:], q_hi[par][:], ALU.subtract).then_inc(ql_done, 1)
                pool.tensor_tensor(qm_hi[par][:], q_hi[par][:], mask_b[bp][:], ALU.mult).then_inc(ql_done, 1)
                upto(pool, ql_done, 2 * (w + 1))
                pool.tensor_tensor(qm_lo[par][:], q_lo[par][:], mask_b[bp][:], ALU.mult).then_inc(q_split, 1)
            if n % 2 == 1 and known(i, n, 5):
                w = 2 * i + (n + 5) // 2
                bp = (n + 5) // 2 % 2
                pool.wait_ge(xhi_done, w + 1)
                pool.tensor_tensor(x_lo[:], x_f[bp][:], x_hi[:], ALU.subtract).then_inc(x_split, 1)

        pool.wait_ge(xhi_done, 1)
        pool.tensor_tensor(x_lo[:], x_f[0][:], x_hi[:], ALU.subtract).then_inc(x_split, 1)
        run_units(pool, step, -4, 2)

    @block.scalar
    def _(act):
        def copy_numerators(i, n):
            w, par = RING * i + n - 1, (n - 1) % 2
            act.wait_ge(num_mm, KB * (w + 1))
            upto(act, c_done, w - 1)
            act.activation(num[par][:], ps_num[:, :], ACT.Copy).then_inc(num_done, 1)

        def copy_denominators(i, n):
            w, par = RING * i + n - 1, (n - 1) % 2
            act.wait_ge(den_mm, 2 * (w + 1))
            act.activation(den[par][:], ps_den[:, :], ACT.Copy).then_inc(den_done, 1)

        def context_high(i, n):
            w = RING * i + n - 2
            act.wait_ge(c_done, w + 1)
            upto(act, o_mm, KT * (2 * i + (n - 2) // 2 - 1))
            act.activation(c_hi[(n - 2) % RING][:], c_f[n % 2][:], ACT.Copy).then_inc(chi_done, 1)

        def copy_maxima(i, n):
            act.wait_ge(mt_mm, RING * i + n + 2)
            if known(i, n, -1):
                act.wait_ge(maxrow_in[(n - 1) % RING], 16 * (i + (n - 1) // RING + 1))
            act.activation(maxrow[(n + 1) % 2][:, :], ps_o[0:HG * KB, 0:P], ACT.Copy, scale=-1.0).then_inc(mt_done, 1)

        def copy_values(i, n):
            w, slot = RING * i + n + 3, (n + 3) % RING
            act.wait_ge(v_mm, w + 1)
            upto(act, num_mm, KB * (w - RING + 1))
            act.activation(v[slot][:].rearrange("p k g d -> p k d g"),
                           ps_q[:, :].rearrange("p (k d g) -> p k d g", k=KB, g=HG), ACT.Copy).then_inc(v_done, 1)

        def copy_q(i, n, high):
            w, par = RING * i + n + 4, n % 2
            if not high:
                act.wait_ge(q_mm, w + 1)
                upto(act, v_mm, w - 1)
                upto(act, q_split, w - 1)
                if known(i, n, 2):
                    act.wait_ge(stack_in[(n + 2) % RING], 16 * STACK_DMAS * (i + 1 + (n + 2) // RING))
            act.activation((q_f, q_hi)[high][par][:], ps_q[:, :], ACT.Copy).then_inc(q_done, 1)

        def copy_out_rows(i, n, half):
            b = 2 * i + (n - 3) // 2
            act.wait_ge(o_mm, KT * b + half + 1)
            upto(act, stored[half], 16 * b)
            upto(act, xt_mm, KT * (b - 1) + half + 1)
            act.activation(xo[half][:], ps_o[:, :], ACT.Copy).then_inc(o_done, 1)

        def copy_turned_rows(i, n, half):
            b = 2 * i + (n - 4) // 2
            act.wait_ge(xt_mm, KT * b + half + 1)
            upto(act, partial_mm, b)
            act.activation(xo_t[:, :, half * P:(half + 1) * P], ps_o[:, :].rearrange("p (k d) -> p k d", k=KB), ACT.Copy).then_inc(xt_done, 1)

        def copy_partial(i, n):
            b = 2 * i + (n - 4) // 2
            act.wait_ge(partial_mm, b + 1)
            upto(act, lg_mm, b)
            act.activation(partial[:], ps_o[:, 0:KT * P], ACT.Copy).then_inc(partial_done, 1)

        def x_high(i, n):
            w, bp = 2 * i + (n + 5) // 2, (n + 5) // 2 % 2
            act.wait_ge(x_in[bp], 16 * (i + (n + 5) // 4 + 1))
            upto(act, q_mm, UPB * w)
            upto(act, x_split, w)
            act.activation(x_hi[:], x_f[bp][:], ACT.Copy).then_inc(xhi_done, 1)

        def weights(i, n, kb, g):
            u = RING * i + n
            if g == 0 and kb % 2 == 0:
                upto(act, den_mm, 2 * (u - 1) + 1 + kb // 2)
            act.wait_ge(e_mm, (KB * u + kb) * HG + g + 1)
            act.activation(e[kb][:, g, :], ps_e[g % 2][:, :], ACT.Exp, scale=SCALE).then_inc(e_done, 1)

        def step(i, n):
            even, odd = n % 2 == 0, n % 2 == 1
            if isinstance(i, int) and RING * i + n == 0:
                act.wait_ge(w_split, 4)
            for kb in range(KB):
                if kb == 1 and known(i, n, -1):
                    copy_numerators(i, n)
                if kb == 2 and known(i, n, -1):
                    copy_denominators(i, n)
                for g in range(HG):
                    if known(i, n):
                        weights(i, n, kb, g)
                    if (kb, g) == (0, 1) and known(i, n, -2):
                        context_high(i, n)
                    if (kb, g) == (0, 3) and known(i, n, 1):
                        copy_maxima(i, n)
                    if (kb, g) == (1, 1) and known(i, n, 3):
                        copy_values(i, n)
                    if kb in (1, 2) and g == 3 and even and known(i, n, -4, hi=NU):
                        copy_turned_rows(i, n, kb - 1)
                    if kb == 2 and g in (1, 2) and known(i, n, 4):
                        copy_q(i, n, g - 1)
                    if kb >= 2 and g == 3 and odd and known(i, n, -3, hi=NU):
                        copy_out_rows(i, n, kb - 2)
                    if (kb, g) == (3, 1) and even and known(i, n, -4, hi=NU):
                        copy_partial(i, n)
                    if (kb, g) == (3, 1) and odd and known(i, n, 5):
                        x_high(i, n)

        act.wait_ge(x_in[0], 16)
        act.activation(x_hi[:], x_f[0][:], ACT.Copy).then_inc(xhi_done, 1)
        run_units(act, step, -4, 5)

    @block.vector
    def _(dve):
        def normalise(i, n, at):
            w, par = RING * i + n - 1, (n - 1) % 2
            if at < 0:
                return
            if at < PARTS:
                c = slice(at * T // PARTS, (at + 1) * T // PARTS)
                if at == 0:
                    dve.wait_ge(den_done, w + 1)
                    upto(dve, c_done, w)
                dve.reciprocal(den[par][:, c], den[par][:, c]).then_inc(rd_done, 1)
            elif at == PARTS:
                dve.wait_ge(rd_done, PARTS * (w + 1))
                dve.wait_ge(num_done, w + 1)
                upto(dve, c_split, w - 1)
                dve.tensor_tensor(c_f[par][:], num[par][:], den[par][:], ALU.mult).then_inc(c_done, 1)

        dve.memset(one_f[:], 1.0).then_inc(dve_set, 1)
        dve.wait_ge(dve_set, 1)
        dve.tensor_copy(one_row[:], one_f[:]).then_inc(setup, 1)
        dve.wait_ge(w_in, 32)
        dve.tensor_copy(wq_hi[:], wq_f).then_inc(w_split, 1)
        dve.tensor_copy(wo_hi[:], wo_f).then_inc(w_split, 1)
        dve.wait_ge(w_split, 2)
        dve.tensor_tensor(wq_lo[:], wq_f, wq_hi[:], ALU.subtract).then_inc(w_split, 1)
        dve.tensor_tensor(wo_lo[:], wo_f, wo_hi[:], ALU.subtract).then_inc(w_split, 1)

        def step(i, n):
            u = RING * i + n
            if n % 2 == 0 and known(i, n, 4):
                b, bp = 2 * i + (n + 4) // 2, n // 2
                dve.wait_ge(mask_in[bp], 16 * (i + 2))
                if known(i, n, 1):
                    dve.wait_ge(stack_in[(n + 1) % RING], 16 * STACK_DMAS * (i + (n + 1) // RING + 1))
                dve.tensor_copy(row_mask[bp][:], mask_b[bp][0:1, :]).then_inc(rows_done, 1)
                dve.tensor_scalar(row_neg[bp][:], mask_b[bp][0:1, :], -NEG, NEG, ALU.mult, ALU.add).then_inc(rows_done, 1)
            for kb in range(KB):
                for g in range(HG):
                    if known(i, n, 2):
                        w, par = u + 2, n % 2
                        dve.wait_ge(m_mm, (KB * w + kb) * HG + g + 1)
                        if kb == 0 and g == 0:
                            upto(dve, mt_mm, w - 1)
                        dve.reduce_max(maxcol[par][:, g * KB + kb:g * KB + kb + 1], ps_m[g % 2][:, :], AX.X).then_inc(max_done, 1)
                    if g == 1 and kb == 1 and known(i, n, -1):
                        add_pair(dve, u - 1, 1, slice(0, HG // 2), pair_dve)
                    if g % 2 == 1 and known(i, n, -1):
                        normalise(i, n, 2 * kb + g // 2 - KB)
                        if kb == KB - 1 and g == HG - 1:
                            normalise(i, n, PARTS)
                if kb == 3 and n % 2 == 0 and known(i, n, -4, hi=NU):
                    b = 2 * i + (n - 4) // 2
                    dve.wait_ge(lg_mm, b + 1)
                    dve.tensor_copy(keep["logits"][:, bass.ds(KT * b, KT), :],
                                    ps_o[:, KT * P:KT * (P + NE)].rearrange("p (h e) -> p h e", h=KT)).then_inc(lg_done, 1)

        run_units(dve, step, -4, 5)

    @block.tensor
    def _(pe):
        pe.wait_ge(w_split, 4)
        pe.wait_ge(setup, 3)

        def parts(out, a, b, kt):
            terms = [(t, l, r) for t in range(kt) for l, r in ((a[0], b[0]), (a[0], b[1]), (a[1], b[0]))]
            for m, (t, l, r) in enumerate(terms):
                last = nc.tensor.matmul(out, l(t), r(t), start=(m == 0), stop=(m == len(terms) - 1))
            return last

        def numerators(u, n, kb):
            if kb == 0:
                upto(pe, num_done, u)
                upto(pe, v_done, u + 1)
            pe.wait_ge(e_done, (KB * u + kb + 1) * HG)
            for g in range(HG):
                last = nc.tensor.matmul(ps_num[g * DK:(g + 1) * DK, :], v[n % RING][:, kb, g, :], e[kb][:, g, :],
                                        start=(kb == 0), stop=(kb == KB - 1))
            last.then_inc(num_mm, 1)

        def denominators(u, pair):
            if pair == 0:
                upto(pe, den_done, u)
            if pair == 1:
                pe.wait_ge(pair_dve, u + 1)
            pe.wait_ge(pair_pool, 2 * u + pair + 1)
            for g in range(HG):
                last = nc.tensor.matmul(ps_den[g * DK:(g + 1) * DK, :], ones[:, :], e[2 * pair][:, g, :],
                                        start=(pair == 0), stop=(pair == 1))
            last.then_inc(den_mm, 1)

        def turn_values(i, n):
            w, par = RING * i + n + 3, (n + 3) % 2
            pe.wait_ge(q_done, 2 * (w + 1))
            for k in range(KB):
                last = nc.tensor.transpose(ps_q[:, k * P:(k + 1) * P], q_f[par][:, k * P:(k + 1) * P], ident[:, :])
            last.then_inc(v_mm, 1)

        def project(i, n):
            upto(pe, x_split, 2 * i + (n + 4) // 2 + 1)
            upto(pe, v_done, RING * i + n + 4)
            c = slice(n % UPB * P, (n % UPB + 1) * P)
            parts(ps_q[:, :], (lambda t: wq_hi[:, t, c], lambda t: wq_lo[:, t, c]),
                  (lambda t: x_hi[:, t, :], lambda t: x_lo[:, t, :]), KT).then_inc(q_mm, 1)

        def turn_maxima(i, n):
            upto(pe, max_done, (RING * i + n + 2) * KB * HG)
            if n % 2 == 0:
                upto(pe, o_done, KT * (2 * i + (n - 4) // 2 + 1))
            else:
                upto(pe, lg_done, 2 * i + (n - 5) // 2 + 1)
            nc.tensor.transpose(ps_o[0:HG * KB, 0:P], maxcol[(n + 1) % 2][:, :], ident[:, :]).then_inc(mt_mm, 1)

        def turn_rows(i, n, half):
            b = 2 * i + (n - 4) // 2
            upto(pe, o_done, KT * (b + 1))
            if half == 0 and known(i, n, 1):
                pe.wait_ge(mt_done, RING * i + n + 2)
            upto(pe, xt_done, KT * b + half)
            for k in range(KB):
                last = nc.tensor.transpose(ps_o[:, k * P:(k + 1) * P], xo[half][:, k * P:(k + 1) * P], ident[:, :])
            last.then_inc(xt_mm, 1)

        def partial_logits(i, n):
            b = 2 * i + (n - 4) // 2
            pe.wait_ge(xt_done, KT * (b + 1))
            for k in range(KB):
                last = nc.tensor.matmul(ps_o[k * P // KB:(k + 1) * P // KB, 0:KT * P], gate_w[:, k, :], xo_t[:, k, :], start=True, stop=True)
            last.then_inc(partial_mm, 1)

        def logits(i, n):
            pe.wait_ge(partial_done, 2 * i + (n - 4) // 2 + 1)
            for half in range(KT):
                last = nc.tensor.matmul(ps_o[:, KT * P + half * NE:KT * P + (half + 1) * NE], partial[:, half * P:(half + 1) * P],
                                        add_up[:], start=True, stop=True)
            last.then_inc(lg_mm, 1)

        def out_rows(i, n, half):
            b = 2 * i + (n - 3) // 2
            upto(pe, c_split, UPB * (b + 1))
            upto(pe, o_done, KT * b + half)
            if known(i, n, 1):
                pe.wait_ge(mt_done, RING * i + n + 2)
            upto(pe, lg_done, b)
            c = slice(half * P, (half + 1) * P)
            s = (n - 3) // 2 % 2 * UPB
            parts(ps_o[:, :], (lambda t: wo_hi[:, t, c], lambda t: wo_lo[:, t, c]),
                  (lambda t: c_hi[s + t][:, :], lambda t: c_lo[s + t][:, :]), KT).then_inc(o_mm, 1)

        def step(i, n):
            u = RING * i + n
            if isinstance(i, int) and u == 0:
                pe.wait_ge(ones_in, 16 * RING)
                pe.wait_ge(gate_in, 16)
                pe.wait_ge(add_up_done, KB)
            for kb in range(KB):
                cols = slice(kb * P, (kb + 1) * P)
                if kb == 0 and known(i, n):
                    pe.wait_ge(maxrow_in[n % RING], 16 * (i + 1))
                if kb == 0 and known(i, n, 2):
                    pe.wait_ge(stack_in[(n + 2) % RING], 16 * STACK_DMAS * (i + 1 + (n + 2) // RING))
                before = ((u - 1, n - 1, KB - 1) if known(i, n, -1) else None) if kb == 0 else ((u, n, kb - 1) if known(i, n) else None)
                for g in range(HG):
                    if known(i, n):
                        tile = (KB * u + kb) * HG + g
                        upto(pe, e_done, tile - 1)
                        nc.tensor.matmul(ps_e[g % 2][:, :], kside[n][:, g, cols], qside[n][:, g, :], start=True, stop=True).then_inc(e_mm, 1)
                    if known(i, n, 2):
                        s2 = (n + 2) % RING
                        tile = (KB * (u + 2) + kb) * HG + g
                        upto(pe, max_done, tile - 1)
                        nc.tensor.matmul(ps_m[g % 2][:, :], qside[s2][0:MAXROW, g, cols], kside[s2][0:MAXROW, g, :], start=True, stop=True).then_inc(m_mm, 1)
                    if g == 0 and kb == 0 and known(i, n, 3):
                        turn_values(i, n)
                    if g == 0 and kb == 2 and known(i, n, 4):
                        project(i, n)
                    if g == 1 and before:
                        numerators(*before)
                    if g == 2 and kb == 0 and known(i, n, 1):
                        turn_maxima(i, n)
                    if g == 2 and kb in (1, 2) and n % 2 == 0 and known(i, n, -4, hi=NU):
                        turn_rows(i, n, kb - 1)
                    if g == 0 and kb == 3 and n % 2 == 0 and known(i, n, -4, hi=NU):
                        partial_logits(i, n)
                    if g == 2 and kb == 3 and n % 2 == 0 and known(i, n, -4, hi=NU):
                        logits(i, n)
                    if g == 2 and kb >= 2 and n % 2 == 1 and known(i, n, -3, hi=NU):
                        out_rows(i, n, kb - 2)
                    if g == 3 and kb == 1 and known(i, n, -1):
                        denominators(u - 1, 1)
                    if g == 3 and kb == 3 and known(i, n):
                        denominators(u, 0)

        run_units(pe, step, -4, 5)


def experts(nc, ctx, sems, keep, attn, w_gate, w_up, w_down, routed):
    import concourse.bass as bass
    from concourse import mybir

    f32, f32r, u32 = mybir.dt.float32, mybir.dt.float32r, mybir.dt.uint32
    ALU, ACT, AX = mybir.AluOpType, mybir.ActivationFunctionType, mybir.AxisListType
    P = 128
    NE, H, I = w_gate.shape
    HT = H // P
    ST = keep["slot_tile"]
    SB = ST // P
    NTILES = routed.shape[0] // ST
    NCOL = routed.shape[0] // P
    NBLK = attn.shape[0] // P
    TOPK = 2
    FEWEST = attn.shape[0] * TOPK // ST
    ROUND = 1.5 * 2 ** 23
    IT = [(lo, min(P, I - lo)) for lo in range(0, I, P)]
    NI = len(IT)
    FULL = I // P

    def sb(name, shape, dt):
        return ctx.enter_context(nc.sbuf_tensor("e_" + name, shape, dt))

    def bank(name, shape):
        return ctx.enter_context(nc.psum_tensor("e_" + name, shape, f32))

    def sem(name):
        return sems.enter_context(nc.semaphore("e_" + name))

    ident = sb("ident", [P, P], f32)
    raw = [sb("raw_g", [P, HT, I], f32), sb("raw_u", [P, HT, I], f32), sb("raw_d", [P, NI, H], f32)]
    hi = [[sb(f"hi_{w}{n}", raw[k].shape, f32r) for k, w in enumerate("gud")] for n in range(2)]
    lo = [[sb(f"lo_{w}{n}", raw[k].shape, f32r) for k, w in enumerate("gud")] for n in range(2)]
    token_of = sb("token_of", [P, NCOL], u32)
    now = sb("now", [P, SB], u32)
    rows = sb("rows", [P, SB, H], f32)
    x_hi, x_lo = sb("x_hi", [P, HT, ST], f32r), sb("x_lo", [P, HT, ST], f32r)
    silu = [sb(f"silu{n}", [P, ST], f32) for n in range(NI)]
    h_f = [sb(f"h_f{n}", [P, ST], f32) for n in range(NI)]
    h_hi = [sb(f"h_hi{n}", [P, ST], f32r) for n in range(NI)]
    h_lo = [sb(f"h_lo{n}", [P, ST], f32r) for n in range(NI)]
    zeros = sb("zeros", [P, SB, H], f32)
    y = sb("y", [P, SB, H], f32)
    before, every = sb("before", [P, P], f32), sb("every", [P, P], f32)
    iota_e, iota_r, iota_c = sb("iota_e", [P, NE], f32), sb("iota_r", [P, P], f32), sb("iota_c", [P, NCOL], f32)
    token = sb("token", [P, TOPK, NBLK], f32)
    big = {n: sb(n, [P, NBLK, NE], f32) for n in ("shifted", "expd", "prob", "eq", "cand", "rest", "one1", "one2",
                                                   "both", "rank", "count", "scan0", "scan1", "place", "pick")}
    row = {n: sb(n, [P, NBLK], f32) for n in ("mx", "sum", "inv", "m1", "m2", "i1", "i2", "ws", "wi", "sge", "sgd", "pf")}
    small = {n: sb(n, [P, NE], f32) for n in ("total", "tiles", "cs0", "cs1", "cs2", "start")}
    bounds_f = sb("bounds_f", [P, NE + 1], f32)
    slot_row, slot_col = sb("slot_row", [P, TOPK, NBLK], f32), sb("slot_col", [P, TOPK, NBLK], f32)
    RO = 4
    ROUNDS = TOPK * NBLK // RO
    is_row = [sb(f"is_row{n}", [P, RO, P], f32r) for n in range(2)]
    token_at = [sb(f"token_at{n}", [P, RO, NCOL], f32r) for n in range(2)]
    ps_r = bank("ps_r", [P, 2, NBLK, NE])
    ps_id = ps_r[:].rearrange("p a b e -> p (a b e)")[:, 0:NCOL]
    ps_t = [bank(f"ps_t{n}", [P, HT // 2, ST]) for n in range(2)]
    ps_h = [bank(f"ps_h{n}", [P, 2, ST]) for n in range(NI)]
    ps_y = [bank(f"ps_y{n}", [P, H]) for n in range(SB)]

    chain, shifted, expd, both, ranked, copied, bounds_done = (sem(n) for n in (
        "chain", "shifted", "expd", "both", "ranked", "copied", "bounds_done"))
    row_hot, col_hot, token_hot, id_mm, ids_done = (sem(n) for n in ("row_hot", "col_hot", "token_hot", "id_mm", "ids_done"))
    base, consts, raw_in = sem("base"), sem("consts"), sem("raw_in")
    hi_done, lo_done = sem("hi_done"), sem("lo_done")
    now_done, rows_in = sem("now_done"), sem("rows_in")
    t_mm, h_mm, y_mm = sem("t_mm"), sem("h_mm"), sem("y_mm")
    xhi_done, xlo_done = sem("xhi_done"), sem("xlo_done")
    silu_done, h_done, hhi_done, h_split = sem("silu_done"), sem("h_done"), sem("hhi_done"), sem("h_split")
    y_done, stored = sem("y_done"), sem("stored")
    filled = sem("filled")
    NPARTS = 4

    def pieces(n):
        for k in range(2):
            yield lambda t, k=k: t[k][:, :, :]
        yield lambda t: t[2][:, 0:FULL, :]
        yield lambda t: t[2][0:I - FULL * P, FULL, :]

    def alone(eng, s, value, met, met_value):
        if not isinstance(value, int):
            value = eng.to_reg(value)
            eng.wait_ge(met, met_value)
        eng.wait_ge(s, value)

    def each_expert(eng, start, tile):
        def one(e, n):
            first = eng.value_load(keep["bounds"][0:1, bass.ds(e, 1)], min_val=0, max_val=NTILES - 2)
            last = eng.value_load(keep["bounds"][0:1, bass.ds(e + 1, 1)], min_val=1, max_val=NTILES - 1)
            start(e, n, first)
            with eng.Fori(first, last) as j:
                tile(j, n)

        with eng.Fori(0, NE // 2 - 1) as pair:
            for n in range(2):
                one(2 * pair + n, n)
        for n in range(2):
            one(NE - 2 + n, n)

    def exists(e):
        return not isinstance(e, int) or e < NE

    def each(ap, width):
        return ap.rearrange("p (c a) -> p c a", a=1).to_broadcast([P, RO, width])

    def same(ap, width):
        return ap.rearrange("p (a w) -> p a w", a=1).to_broadcast([P, RO, width])

    def rounds(eng, step):
        for m in range(2):
            step(m, m)
        with eng.Fori(1, ROUNDS // 2 - 1) as i:
            for n in range(2):
                step(2 * i + n, n)
        for m in range(ROUNDS - 2, ROUNDS):
            step(m, m % 2)

    block = ctx.enter_context(nc.Block())

    @block.sync
    def _(sp):
        def load(e):
            for k, w in enumerate((w_gate, w_up)):
                sp.dma_start(raw[k][:], w[bass.ds(e, 1), :, :].rearrange("e (k p) i -> p (e k) i", p=P)).then_inc(raw_in, 16)
            sp.dma_start(raw[2][:, 0:FULL, :], w_down[bass.ds(e, 1), 0:FULL * P, :].rearrange("e (k p) h -> p (e k) h", p=P)).then_inc(raw_in, 16)
            sp.dma_start(raw[2][0:I - FULL * P, FULL, :], w_down[bass.ds(e, 1), FULL * P:I, :].rearrange("e p h -> p (e h)")).then_inc(raw_in, 16)

        load(0)
        sp.wait_ge(consts, 8)
        for j in range(FEWEST, NTILES):
            sp.dma_start(routed[j * ST:(j + 1) * ST, :].rearrange("(s p) h -> p s h", p=P), zeros[:]).then_inc(filled, 16)
        sp.wait_ge(lo_done, NPARTS)
        load(1)
        sp.wait_ge(filled, 16 * (NTILES - FEWEST))
        sp.wait_ge(bounds_done, 1)

        def start(e, n, first):
            if exists(e + 2):
                sp.wait_ge(lo_done, NPARTS * (e + 2))
                load(e + 2)

        def tile(j, n):
            sp.wait_ge(y_done, SB * (j + 1) + SB)
            sp.dma_start(routed[bass.ds(j * ST, ST), :].rearrange("(s p) h -> p s h", p=P), y[:]).then_inc(stored, 16)

        each_expert(sp, start, tile)
        total = sp.value_load(keep["bounds"][0:1, NE:NE + 1], min_val=1, max_val=NTILES - 1)
        keep["load_ahead"](sp)
        alone(sp, stored, 16 * total + 16, consts, 8)

    @block.gpsimd
    def _(pool):
        pool.memset(ident[:], 0.0).then_inc(base, 1)
        pool.memset(before[:], 0.0).then_inc(base, 1)
        pool.iota(iota_e[:], pattern=[[1, NE]], base=0, channel_multiplier=0, allow_small_or_imprecise_dtypes=True).then_inc(consts, 1)
        pool.wait_ge(base, 2)
        pool.affine_select(out=before[:], in_=before[:], compare_op=ALU.is_ge, fill=1.0, base=0,
                           pattern=[[-1, P]], channel_multiplier=1).then_inc(consts, 1)
        pool.memset(every[:], 1.0).then_inc(consts, 1)
        pool.affine_select(out=ident[:], in_=ident[:], compare_op=ALU.not_equal, fill=1.0, base=0,
                           pattern=[[-1, P]], channel_multiplier=1).then_inc(consts, 1)
        for tile in (iota_r, iota_c):
            pool.iota(tile[:], pattern=[[1, tile.shape[1]]], base=0, channel_multiplier=0,
                      allow_small_or_imprecise_dtypes=True).then_inc(consts, 1)
        pool.iota(token[:], pattern=[[0, TOPK], [P, NBLK]], base=0, channel_multiplier=1,
                  allow_small_or_imprecise_dtypes=True).then_inc(consts, 1)
        pool.memset(zeros[:], 0.0).then_inc(consts, 1)

        def times_token(m, n):
            pool.wait_ge(col_hot, m + 1)
            of = token[:].rearrange("p k b -> p (k b)")[:, bass.ds(RO * m, RO)]
            pool.tensor_tensor(token_at[n][:], token_at[n][:], each(of, NCOL), ALU.mult).then_inc(token_hot, 1)

        rounds(pool, times_token)
        pool.wait_ge(bounds_done, 1)
        pool.wait_ge(ids_done, 1)

        def gather(j):
            pool.tensor_copy(now[:], token_of[:, bass.ds(j * SB, SB)]).then_inc(now_done, 1)
            alone(pool, now_done, j + 1, ids_done, 1)
            for s in range(SB):
                pool.indirect_dma_start(out=rows[:, s, :], out_offset=None, in_=attn,
                                        in_offset=bass.IndirectOffsetOnAxis(ap=now[:, s:s + 1], axis=0)).then_inc(rows_in, 16)

        gather(0)

        def tile(j, n):
            pool.wait_ge(rows_in, 16 * SB * (j + 1))
            pool.wait_ge(t_mm, 2 * (j + 1))
            gather(j + 1)

        each_expert(pool, lambda e, n, first: None, tile)
        total = pool.value_load(keep["bounds"][0:1, NE:NE + 1], min_val=1, max_val=NTILES - 1)
        pool.wait_ge(rows_in, 16 * SB * (total + 1))

    @block.scalar
    def _(act):
        def split(e, n):
            act.wait_ge(raw_in, 16 * NPARTS * (e + 1))
            for part in pieces(n):
                act.activation(part(hi[n]), part(raw), ACT.Copy).then_inc(hi_done, 1)

        def x_high(j):
            for a in range(2):
                act.wait_ge(t_mm, 2 * j + a + 1)
                act.activation(x_hi[:, a * HT // 2:(a + 1) * HT // 2, :], ps_t[a][:], ACT.Copy).then_inc(xhi_done, 1)

        act.wait_ge(shifted, 1)
        act.activation(big["expd"][:], big["shifted"][:], ACT.Exp).then_inc(expd, 1)
        act.activation(row["sge"][:], keep["logits"][:, :, NE], ACT.Exp, scale=-1.0).then_inc(expd, 1)
        act.sem_inc(y_done, SB)
        act.sem_inc(stored, 16)
        split(0, 0)
        x_high(0)
        act.wait_ge(bounds_done, 1)

        def start(e, n, first):
            if exists(e + 1):
                act.wait_ge(y_mm, SB * first + SB)
                split(e + 1, 1 - n)

        def tile(j, n):
            for t, (_, width) in enumerate(IT):
                act.wait_ge(h_mm, NI * j + t + 1)
                act.wait_ge(h_done, NI * j + t + 1)
                act.activation(silu[t][0:width, :], ps_h[t][0:width, 0, :], ACT.Silu).then_inc(silu_done, 1)
            x_high(j + 1)
            for s in range(SB):
                act.wait_ge(y_mm, SB * j + s + 1 + SB)
                if s == 0:
                    act.wait_ge(stored, 16 * (j + 1))
                act.activation(y[:, s, :], ps_y[s][:], ACT.Copy).then_inc(y_done, 1)

        each_expert(act, start, tile)


    @block.vector
    def _(dve):
        def split(e, n):
            for k, part in enumerate(pieces(n)):
                dve.wait_ge(hi_done, NPARTS * e + k + 1)
                dve.tensor_tensor(part(lo[n]), part(raw), part(hi[n]), ALU.subtract).then_inc(lo_done, 1)

        def x_low(j):
            for a in range(2):
                dve.wait_ge(xhi_done, 2 * j + a + 1)
                ks = slice(a * HT // 2, (a + 1) * HT // 2)
                dve.tensor_tensor(x_lo[:, ks, :], ps_t[a][:], x_hi[:, ks, :], ALU.subtract).then_inc(xlo_done, 1)

        dve.wait_ge(consts, 8)
        done = [0]

        def link(ins):
            done[0] += 1
            ins.then_inc(chain, 1)
            dve.wait_ge(chain, done[0])

        def wide(ap):
            return ap.rearrange("p (b a) -> p b a", a=1).to_broadcast([P, NBLK, NE])

        def narrow(ap):
            return ap.rearrange("p (a e) -> p a e", a=1).to_broadcast([P, NBLK, NE])

        B, R, S = big, row, small
        link(dve.reduce_max(R["mx"][:], keep["logits"][:, :, 0:NE], AX.X))
        dve.tensor_tensor(B["shifted"][:], keep["logits"][:, :, 0:NE], wide(R["mx"][:]), ALU.subtract).then_inc(shifted, 1)
        dve.wait_ge(expd, 2)
        link(dve.reduce_sum(R["sum"][:], B["expd"][:], AX.X))
        link(dve.reciprocal(R["inv"][:], R["sum"][:]))
        link(dve.tensor_tensor(B["prob"][:], B["expd"][:], wide(R["inv"][:]), ALU.mult))
        src = "prob"
        for m, ind, one, k in (("m1", "i1", "one1", 0), ("m2", "i2", "one2", 1)):
            link(dve.reduce_max(R[m][:], B[src][:], AX.X))
            link(dve.tensor_tensor(B["eq"][:], B[src][:], wide(R[m][:]), ALU.is_equal))
            link(dve.tensor_scalar(B["cand"][:], B["eq"][:], -float(NE), None, ALU.mult))
            link(dve.tensor_tensor(B["cand"][:], B["cand"][:], narrow(iota_e[:]), ALU.add))
            link(dve.tensor_reduce(R[ind][:], B["cand"][:], AX.X, ALU.min))
            link(dve.tensor_scalar(R[ind][:], R[ind][:], float(NE), None, ALU.add))
            link(dve.tensor_tensor(B[one][:], narrow(iota_e[:]), wide(R[ind][:]), ALU.is_equal))
            if k == 0:
                link(dve.tensor_scalar(B["cand"][:], B["one1"][:], -2.0, None, ALU.mult))
                link(dve.tensor_tensor(B["rest"][:], B["prob"][:], B["cand"][:], ALU.add))
                src = "rest"
        dve.tensor_tensor(B["both"][:], B["one1"][:], B["one2"][:], ALU.add).then_inc(both, 1)
        link(dve.tensor_tensor(R["ws"][:], R["m1"][:], R["m2"][:], ALU.add))
        link(dve.reciprocal(R["wi"][:], R["ws"][:]))
        link(dve.tensor_tensor(keep["weight"][:, 0, :], R["m1"][:], R["wi"][:], ALU.mult))
        link(dve.tensor_tensor(keep["weight"][:, 1, :], R["m2"][:], R["wi"][:], ALU.mult))
        link(dve.tensor_scalar(R["sgd"][:], R["sge"][:], 1.0, None, ALU.add))
        link(dve.reciprocal(keep["shared_gate"][:], R["sgd"][:]))
        dve.wait_ge(ranked, 2)
        dve.tensor_copy(B["rank"][:], ps_r[:, 0]).then_inc(copied, 1)
        dve.tensor_copy(B["count"][:], ps_r[:, 1]).then_inc(copied, 1)
        dve.wait_ge(copied, 2)
        link(dve.tensor_copy(B["scan0"][:], B["count"][:]))
        a, b, d = "scan0", "scan1", 1
        while d < NBLK:
            link(dve.tensor_copy(B[b][:, 0:d, :], B[a][:, 0:d, :]))
            link(dve.tensor_tensor(B[b][:, d:, :], B[a][:, d:, :], B[a][:, 0:NBLK - d, :], ALU.add))
            a, b, d = b, a, 2 * d
        link(dve.tensor_scalar(S["total"][:], B[a][:, NBLK - 1, :], 1.0 / ST, (ST - 1.0) / ST - 0.5 + 0.25 / ST, ALU.mult, ALU.add))
        link(dve.tensor_scalar(S["tiles"][:], S["total"][:], ROUND, -ROUND, ALU.add, ALU.add))
        link(dve.tensor_scalar(S["tiles"][:], S["tiles"][:], 1.0, None, ALU.max))
        c, e, d = "tiles", "cs0", 1
        while d < NE:
            link(dve.tensor_copy(S[e][:, 0:d], S[c][:, 0:d]))
            link(dve.tensor_tensor(S[e][:, d:], S[c][:, d:], S[c][:, 0:NE - d], ALU.add))
            c, e, d = e, {"cs0": "cs1", "cs1": "cs2"}.get(e), 2 * d
        link(dve.memset(bounds_f[:, 0:1], 0.0))
        link(dve.tensor_copy(bounds_f[:, 1:], S[c][:]))
        dve.tensor_copy(keep["bounds"][:], bounds_f[:]).then_inc(bounds_done, 1)
        link(dve.tensor_scalar(S["start"][:], bounds_f[:, 0:NE], float(ST), None, ALU.mult))
        link(dve.tensor_tensor(B["place"][:], B[a][:], B["count"][:], ALU.subtract))
        link(dve.tensor_tensor(B["place"][:], B["place"][:], B["rank"][:], ALU.add))
        link(dve.tensor_tensor(B["place"][:], B["place"][:], narrow(S["start"][:]), ALU.add))
        for k, one in enumerate(("one1", "one2")):
            link(dve.tensor_tensor(B["pick"][:], B["place"][:], B[one][:], ALU.mult))
            link(dve.reduce_sum(R["pf"][:], B["pick"][:], AX.X))
            link(dve.tensor_copy(keep["slot"][:, k, :], R["pf"][:]))
            link(dve.tensor_scalar(slot_col[:, k, :], R["pf"][:], 1.0 / P, -0.5 + 0.5 / P, ALU.mult, ALU.add))
            link(dve.tensor_scalar(slot_col[:, k, :], slot_col[:, k, :], ROUND, -ROUND, ALU.add, ALU.add))
            link(dve.tensor_scalar(slot_row[:, k, :], slot_col[:, k, :], -float(P), None, ALU.mult))
            link(dve.tensor_tensor(slot_row[:, k, :], slot_row[:, k, :], R["pf"][:], ALU.add))

        def hot_ones(m, n):
            if not isinstance(m, int) or m >= 2:
                dve.wait_ge(id_mm, RO * (m - 1))
            of = bass.ds(RO * m, RO)
            dve.tensor_tensor(token_at[n][:], same(iota_c[:], NCOL), each(slot_col[:].rearrange("p k b -> p (k b)")[:, of], NCOL),
                              ALU.is_equal).then_inc(col_hot, 1)
            dve.tensor_tensor(is_row[n][:], same(iota_r[:], P), each(slot_row[:].rearrange("p k b -> p (k b)")[:, of], P),
                              ALU.is_equal).then_inc(row_hot, 1)

        rounds(dve, hot_ones)
        dve.wait_ge(id_mm, TOPK * NBLK)
        dve.tensor_copy(token_of[:], ps_id).then_inc(ids_done, 1)

        dve.sem_inc(h_done, NI)
        split(0, 0)
        x_low(0)

        def start(e, n, first):
            if exists(e + 1):
                split(e + 1, 1 - n)

        def tile(j, n):
            for t, (_, width) in enumerate(IT):
                w = slice(0, width)
                dve.wait_ge(silu_done, NI * j + t + 1)
                dve.tensor_tensor(h_f[t][w, :], silu[t][w, :], ps_h[t][w, 1, :], ALU.mult).then_inc(h_done, 1)
                dve.wait_ge(h_done, NI * j + t + 1 + NI)
                dve.tensor_copy(h_hi[t][w, :], h_f[t][w, :]).then_inc(hhi_done, 1)
                dve.wait_ge(hhi_done, NI * j + t + 1)
                dve.tensor_tensor(h_lo[t][w, :], h_f[t][w, :], h_hi[t][w, :], ALU.subtract).then_inc(h_split, 1)
            x_low(j + 1)

        each_expert(dve, start, tile)

    @block.tensor
    def _(pe):
        pe.wait_ge(consts, 8)
        pe.wait_ge(both, 1)
        pairs = big["both"][:].rearrange("p b e -> p (b e)")
        for k, left in enumerate((before, every)):
            nc.tensor.matmul(ps_r[:, k].rearrange("p b e -> p (b e)"), left[:], pairs, start=True, stop=True).then_inc(ranked, 1)

        def place_tokens(m, n):
            pe.wait_ge(row_hot, m + 1)
            pe.wait_ge(token_hot, m + 1)
            for c in range(RO):
                nc.tensor.matmul(ps_id, is_row[n][:, c, :], token_at[n][:, c, :], start=(isinstance(m, int) and m + c == 0),
                                 stop=(isinstance(m, int) and m + 1 == ROUNDS and c == RO - 1)).then_inc(id_mm, 1)

        pe.wait_ge(copied, 2)
        rounds(pe, place_tokens)
        pe.wait_ge(bounds_done, 1)
        pe.sem_inc(y_mm, SB)

        def turn(j):
            pe.wait_ge(rows_in, 16 * SB * (j + 1))
            for a in range(2):
                for m in range(HT // 2):
                    k = a * HT // 2 + m
                    for s in range(SB):
                        last = nc.tensor.transpose(ps_t[a][:, m, s * P:(s + 1) * P], rows[:, s, k * P:(k + 1) * P], ident[:])
                last.then_inc(t_mm, 1)

        turn(0)

        def start(e, n, first):
            alone(pe, lo_done, NPARTS * (e + 1), consts, 8)

        def tile(j, n):
            pe.wait_ge(xlo_done, 2 * (j + 1))
            for t, (at, width) in enumerate(IT):
                pe.wait_ge(h_done, NI * j + t + 1)
                for k in range(2):
                    terms = [(m, l, r) for m in range(HT) for l, r in ((hi[n], x_hi), (hi[n], x_lo), (lo[n], x_hi))]
                    for c, (m, l, r) in enumerate(terms):
                        last = nc.tensor.matmul(ps_h[t][0:width, k, :], l[k][:, m, at:at + width], r[:, m, :],
                                                start=(c == 0), stop=(c == len(terms) - 1))
                last.then_inc(h_mm, 1)
            turn(j + 1)
            for t, (_, width) in enumerate(IT):
                pe.wait_ge(h_split, NI * j + t + 1)
                w = slice(0, width)
                for s in range(SB):
                    if t == 0:
                        pe.wait_ge(y_done, SB * j + s + 1)
                    c = slice(s * P, (s + 1) * P)
                    for m, (l, r) in enumerate(((h_hi, hi[n]), (h_hi, lo[n]), (h_lo, hi[n]))):
                        last = nc.tensor.matmul(ps_y[s][:], l[t][w, c], r[2][w, t, :],
                                                start=(t == 0 and m == 0), stop=(t == NI - 1 and m == 2))
                    if t == NI - 1:
                        last.then_inc(y_mm, 1)

        each_expert(pe, start, tile)


def load_rows(sp, ahead, attn, g):
    import concourse.bass as bass

    _, blocks, _ = ahead["rows"].shape
    sp.dma_start(ahead["rows"][:], attn[bass.ds(g * blocks * 128, blocks * 128), :].rearrange("(s p) h -> p s h", p=128)).then_inc(ahead["rows_in"], 16)


def load_chunk(sp, ahead, sw_gate, sw_up, sw_down, t):
    c = slice(t * 128, (t + 1) * 128)
    arrived = ahead["raw_in"][t % 2]
    for k, w in enumerate((sw_gate, sw_up)):
        sp.dma_start(ahead["raw_gu"][t % 2][:, k, :, :], w[:, c].rearrange("(k p) i -> p k i", p=128)).then_inc(arrived, 16)
    sp.dma_start(ahead["raw_d"][t % 2][:], sw_down[c, :]).then_inc(arrived, 16)


def shared(nc, ctx, sems, keep, x, attn, sw_gate, sw_up, sw_down, routed, out):
    import concourse.bass as bass
    from concourse import mybir

    f32, f32r, u32 = mybir.dt.float32, mybir.dt.float32r, mybir.dt.uint32
    ALU, ACT = mybir.AluOpType, mybir.ActivationFunctionType
    P = 128
    NTOK, H = attn.shape
    I = sw_gate.shape[1]
    HT, NI = H // P, I // P
    GT = 512
    GB = GT // P
    NG = NTOK // GT
    TOPK = 2

    def sb(name, shape, dt):
        return ctx.enter_context(nc.sbuf_tensor("s_" + name, shape, dt))

    def bank(name):
        return ctx.enter_context(nc.psum_tensor("s_" + name, [P, 512], f32))

    def sem(name):
        return sems.enter_context(nc.semaphore("s_" + name))

    ident = sb("ident", [P, P], f32)
    raw_gu, raw_d, raw_in, rows, rows_in = (keep["ahead"][n] for n in ("raw_gu", "raw_d", "raw_in", "rows", "rows_in"))
    gu_hi, gu_lo = sb("gu_hi", [P, NI, 2, HT, P], f32r), sb("gu_lo", [P, NI, 2, HT, P], f32r)
    d_hi, d_lo = sb("d_hi", [P, NI, H], f32r), sb("d_lo", [P, NI, H], f32r)
    x_hi, x_lo = sb("x_hi", [P, HT, GT], f32r), sb("x_lo", [P, HT, GT], f32r)
    silu, h_f = sb("silu", [P, GT], f32), sb("h_f", [P, GT], f32)
    h_hi, h_lo = ([sb(f"h_{w}{n}", [P, GT], f32r) for n in range(2)] for w in ("hi", "lo"))
    slot_now, scale_now = sb("slot_now", [P, TOPK, GB], u32), sb("scale_now", [P, TOPK + 1, GB], f32)
    chosen = [[sb(f"chosen{k}{n}", [P, H], f32) for n in range(2)] for k in range(TOPK)]
    total = [sb(f"total{n}", [P, H], f32) for n in range(GB)]
    ps_t = [bank(f"ps_t{n}") for n in range(2)]
    ps_g, ps_u = bank("ps_g"), bank("ps_u")
    ps_y = [bank(f"ps_y{n}") for n in range(GB)]

    base, consts = sem("base"), sem("consts")
    w_hi, w_lo = sem("w_hi"), sem("w_lo")
    residual_in, stored = [sem(f"residual_in{n}") for n in range(GB)], [sem(f"stored{n}") for n in range(GB)]
    chosen_in = [sem(f"chosen_in{n}") for n in range(2)]
    t_mm, g_mm, u_mm, y_mm = sem("t_mm"), sem("g_mm"), sem("u_mm"), sem("y_mm")
    xhi_done, xlo_done = sem("xhi_done"), sem("xlo_done")
    silu_done, h_done, hhi_done, h_split = sem("silu_done"), sem("h_done"), sem("hhi_done"), sem("h_split")
    slot_done, scale_done, y_read, sum_done, out_ready = sem("slot_done"), sem("scale_done"), sem("y_read"), sem("sum_done"), sem("out_ready")

    x_v = x.rearrange("b d t -> (b d) t")
    out_v = out.rearrange("b d t -> (b d) t")

    def upto(eng, s, value):
        if not (isinstance(value, int) and value <= 0):
            eng.wait_ge(s, value)

    def alone(eng, s, value, met, met_value):
        if not isinstance(value, int):
            value = eng.to_reg(value)
            eng.wait_ge(met, met_value)
        eng.wait_ge(s, value)

    def groups(eng, group):
        group(0)
        with eng.Fori(1, NG - 1) as g:
            group(g)
        group(NG - 1)

    def more(g):
        return not isinstance(g, int) or g + 1 < NG

    block = ctx.enter_context(nc.Block())

    @block.sync
    def _(sp):
        for t in range(2, NI):
            sp.wait_ge(w_lo, 2 * (t - 1))
            load_chunk(sp, keep["ahead"], sw_gate, sw_up, sw_down, t)

        def group(g):
            if more(g):
                sp.wait_ge(t_mm, HT * (g + 1))
                load_rows(sp, keep["ahead"], attn, g + 1)
            if not isinstance(g, int) or g:
                store(g - 1)
            for s in range(GB):
                upto(sp, stored[s], 16 * g)
                sp.dma_start(total[s][:], x_v[bass.ds((GB * g + s) * P, P), :]).then_inc(residual_in[s], 16)

        def store(g):
            for s in range(GB):
                b = GB * g + s
                sp.wait_ge(out_ready, b + 1)
                sp.dma_start(out_v[bass.ds(b * P, P), :], total[s][:]).then_inc(stored[s], 16)

        groups(sp, group)
        store(NG - 1)
        for s in range(GB):
            sp.wait_ge(stored[s], 16 * NG)

    @block.gpsimd
    def _(pool):
        pool.memset(ident[:], 0.0).then_inc(base, 1)
        pool.wait_ge(base, 1)
        pool.affine_select(out=ident[:], in_=ident[:], compare_op=ALU.not_equal, fill=1.0, base=0,
                           pattern=[[-1, P]], channel_multiplier=1).then_inc(consts, 1)

        def group(g):
            for n in range(2):
                upto(pool, chosen_in[n], 16 * TOPK * 2 * g)
            pool.tensor_copy(slot_now[:], keep["slot"][:, :, bass.ds(GB * g, GB)]).then_inc(slot_done, 1)
            pool.wait_ge(slot_done, g + 1)
            for s in range(GB):
                b = GB * g + s
                if not (isinstance(b, int) and b <= 1):
                    alone(pool, out_ready, b - 1, consts, 1)
                for k in range(TOPK):
                    pool.indirect_dma_start(out=chosen[k][s % 2][:], out_offset=None, in_=routed,
                                            in_offset=bass.IndirectOffsetOnAxis(ap=slot_now[:, k, s:s + 1], axis=0)).then_inc(chosen_in[s % 2], 16)

        groups(pool, group)

    @block.scalar
    def _(act):
        def x_high(g):
            for m in range(HT):
                act.wait_ge(t_mm, HT * g + m + 1)
                act.activation(x_hi[:, m, :], ps_t[m % 2][:], ACT.Copy).then_inc(xhi_done, 1)

        def split(t):
            act.wait_ge(raw_in[t % 2], 16 * 3 * (t // 2 + 1))
            act.activation(gu_hi[:, t], raw_gu[t % 2][:], ACT.Copy).then_inc(w_hi, 1)
            act.activation(d_hi[:, t], raw_d[t % 2][:], ACT.Copy).then_inc(w_hi, 1)

        def group(g):
            first = isinstance(g, int) and g == 0
            for t in range(NI):
                if first and t + 2 < NI:
                    split(t + 2)
                act.wait_ge(g_mm, NI * g + t + 1)
                upto(act, h_done, NI * g + t)
                act.activation(silu[:], ps_g[:], ACT.Silu).then_inc(silu_done, 1)
            if more(g):
                act.wait_ge(u_mm, NI * (g + 1))
                x_high(g + 1)

        x_high(0)
        split(0)
        split(1)
        groups(act, group)

    @block.vector
    def _(dve):
        def x_low(g):
            for m in range(HT):
                dve.wait_ge(xhi_done, HT * g + m + 1)
                dve.tensor_tensor(x_lo[:, m, :], ps_t[m % 2][:], x_hi[:, m, :], ALU.subtract).then_inc(xlo_done, 1)

        def split(t):
            dve.wait_ge(w_hi, 2 * t + 1)
            dve.tensor_tensor(gu_lo[:, t], raw_gu[t % 2][:], gu_hi[:, t], ALU.subtract).then_inc(w_lo, 1)
            dve.wait_ge(w_hi, 2 * t + 2)
            dve.tensor_tensor(d_lo[:, t], raw_d[t % 2][:], d_hi[:, t], ALU.subtract).then_inc(w_lo, 1)

        def group(g):
            first = isinstance(g, int) and g == 0
            for t in range(NI):
                if first and t + 2 < NI:
                    split(t + 2)
                n = NI * g + t
                dve.wait_ge(silu_done, n + 1)
                dve.wait_ge(u_mm, n + 1)
                upto(dve, h_split, n)
                dve.tensor_tensor(h_f[:], silu[:], ps_u[:], ALU.mult).then_inc(h_done, 1)
                dve.wait_ge(h_done, n + 1)
                upto(dve, y_mm, n if t == 0 else n - 1)
                dve.tensor_copy(h_hi[t % 2][:], h_f[:]).then_inc(hhi_done, 1)
                dve.wait_ge(hhi_done, n + 1)
                dve.tensor_tensor(h_lo[t % 2][:], h_f[:], h_hi[t % 2][:], ALU.subtract).then_inc(h_split, 1)
                if t < GB and (not isinstance(g, int) or g):
                    add_chosen(g - 1, t)
            if more(g):
                x_low(g + 1)
            upto(dve, out_ready, GB * g)
            dve.tensor_copy(scale_now[:, 0:TOPK, :], keep["weight"][:, :, bass.ds(GB * g, GB)]).then_inc(scale_done, 1)
            dve.tensor_copy(scale_now[:, TOPK, :], keep["shared_gate"][:, bass.ds(GB * g, GB)]).then_inc(scale_done, 1)
            dve.wait_ge(scale_done, 2 * (g + 1))
            dve.wait_ge(y_mm, NI * (g + 1))
            for s in range(GB):
                dve.wait_ge(residual_in[s], 16 * (g + 1))
                dve.scalar_tensor_tensor(out=total[s][:], in0=ps_y[s][:], scalar=scale_now[:, TOPK, s:s + 1],
                                         in1=total[s][:], op0=ALU.mult, op1=ALU.add).then_inc(y_read, 1)

        def add_chosen(g, s):
            b = GB * g + s
            dve.wait_ge(chosen_in[s % 2], 16 * TOPK * (2 * g + s // 2 + 1))
            dve.wait_ge(y_read, b + 1)
            dve.scalar_tensor_tensor(out=total[s][:], in0=chosen[0][s % 2][:], scalar=scale_now[:, 0, s:s + 1],
                                     in1=total[s][:], op0=ALU.mult, op1=ALU.add).then_inc(sum_done, 1)
            dve.wait_ge(sum_done, b + 1)
            dve.scalar_tensor_tensor(out=total[s][:], in0=chosen[1][s % 2][:], scalar=scale_now[:, 1, s:s + 1],
                                     in1=total[s][:], op0=ALU.mult, op1=ALU.add).then_inc(out_ready, 1)

        x_low(0)
        split(0)
        split(1)
        groups(dve, group)
        for s in range(GB):
            add_chosen(NG - 1, s)

    @block.tensor
    def _(pe):
        pe.wait_ge(consts, 1)

        def turn(g, m):
            if m == 0:
                pe.wait_ge(rows_in, 16 * (g + 1))
            upto(pe, xlo_done, HT * g + m - 1)
            for s in range(GB):
                last = nc.tensor.transpose(ps_t[m % 2][:, s * P:(s + 1) * P], rows[:, s, m * P:(m + 1) * P], ident[:])
            last.then_inc(t_mm, 1)

        def up(g, t, k, ps, s, mm):
            terms = [(m, l, r) for m in range(HT) for l, r in ((gu_hi, x_hi), (gu_hi, x_lo), (gu_lo, x_hi))]
            for c, (m, l, r) in enumerate(terms):
                last = nc.tensor.matmul(ps[:], l[:, t, k, m, :], r[:, m, :], start=(c == 0), stop=(c == len(terms) - 1))
            last.then_inc(mm, 1)

        def down(g, t):
            n = NI * g + t
            pe.wait_ge(h_split, n + 1)
            for s in range(GB):
                if t == 0:
                    upto(pe, y_read, GB * g - GB + s + 1 if not isinstance(g, int) or g else 0)
                c = slice(s * P, (s + 1) * P)
                for m, (l, r) in enumerate(((h_hi, d_hi), (h_hi, d_lo), (h_lo, d_hi))):
                    last = nc.tensor.matmul(ps_y[s][:], l[t % 2][:, c], r[:, t, :], start=(t == 0 and m == 0), stop=(t == NI - 1 and m == 2))
            last.then_inc(y_mm, 1)

        def group(g):
            first = isinstance(g, int) and g == 0
            for t in range(NI):
                n = NI * g + t
                if t == 0:
                    pe.wait_ge(xlo_done, HT * (g + 1))
                if first:
                    pe.wait_ge(w_lo, 2 * (t + 1))
                if t == NI - 1 and more(g):
                    turn(g + 1, 0)
                    turn(g + 1, 1)
                upto(pe, silu_done, n)
                up(g, t, 0, ps_g, silu_done, g_mm)
                upto(pe, h_done, n)
                up(g, t, 1, ps_u, h_done, u_mm)
                if t:
                    down(g, t - 1)
            if more(g):
                turn(g + 1, 2)
                turn(g + 1, 3)
            down(g, NI - 1)

        for m in range(HT):
            turn(0, m)
        groups(pe, group)


def build(nc, x, mask, wq_t, wo_t, gates, w_gate, w_up, w_down, sw_gate, sw_up, sw_down, out):
    from contextlib import ExitStack
    from concourse import mybir

    f32, i32, u32 = mybir.dt.float32, mybir.dt.int32, mybir.dt.uint32
    P = 128
    NB, D, T = x.shape
    NTOK, NE, TOPK = NB * D, w_gate.shape[0], 2
    SLOT_TILE = 256
    NTILES = NTOK * TOPK // SLOT_TILE + NE + 1
    attn = nc.dram_tensor("attn", (NTOK, T), f32, kind="Internal").ap()
    routed = nc.dram_tensor("routed", (NTILES * SLOT_TILE, T), f32, kind="Internal").ap()

    with ExitStack() as whole:
        def sb(name, shape, dt):
            return whole.enter_context(nc.sbuf_tensor("keep_" + name, shape, dt))

        keep = {
            "slot": sb("slot", [P, TOPK, NTOK // P], u32),
            "logits": sb("logits", [P, NTOK // P, NE + 1], f32),
            "weight": sb("weight", [P, TOPK, NTOK // P], f32),
            "shared_gate": sb("shared_gate", [P, NTOK // P], f32),
            "bounds": sb("bounds", [P, NE + 1], i32),
            "slot_tile": SLOT_TILE,
        }
        with ExitStack() as ctx:
            attention(nc, ctx, whole, keep, x, mask, wq_t, wo_t, gates, attn)
        blocks, hk = 4, sw_gate.shape[0] // P
        keep["ahead"] = {
            "rows": sb("rows", [P, blocks, T], f32),
            "raw_gu": [sb(f"raw_gu{n}", [P, 2, hk, P], f32) for n in range(2)],
            "raw_d": [sb(f"raw_d{n}", [P, T], f32) for n in range(2)],
            "rows_in": whole.enter_context(nc.semaphore("rows_in")),
            "raw_in": [whole.enter_context(nc.semaphore(f"raw_in{n}")) for n in range(2)],
        }

        def load_ahead(sp):
            load_rows(sp, keep["ahead"], attn, 0)
            for t in range(2):
                load_chunk(sp, keep["ahead"], sw_gate, sw_up, sw_down, t)

        keep["load_ahead"] = load_ahead
        with ExitStack() as ctx:
            experts(nc, ctx, whole, keep, attn, w_gate, w_up, w_down, routed)
        with ExitStack() as ctx:
            shared(nc, ctx, whole, keep, x, attn, sw_gate, sw_up, sw_down, routed, out)


def kernel(x, cond_2048, L0_cond_Wq, L0_cond_Wo, L0_ffn_gate_w, L0_ffn_w_gate, L0_ffn_w_up, L0_ffn_w_down,
           L0_ffn_sw_gate, L0_ffn_sw_up, L0_ffn_sw_down, L0_ffn_shared_gate_w):
    import numpy as np
    import concourse.bacc as bacc
    from concourse import mybir
    from concourse.bass_utils import run_bass_kernel_spmd

    D = L0_cond_Wq.shape[0]
    NH, P = 8, 128
    DK = D // NH
    wq_t = np.asarray(L0_cond_Wq).T.reshape(D, D // P, P // DK, DK).transpose(0, 1, 3, 2).reshape(D, D)
    gates = np.concatenate([np.asarray(L0_ffn_gate_w).T, np.asarray(L0_ffn_shared_gate_w)], axis=1)
    arrays = {
        "x": x, "mask": cond_2048, "wq_t": wq_t, "wo_t": np.asarray(L0_cond_Wo).T, "gates": gates,
        "w_gate": L0_ffn_w_gate, "w_up": L0_ffn_w_up, "w_down": L0_ffn_w_down,
        "sw_gate": L0_ffn_sw_gate, "sw_up": L0_ffn_sw_up, "sw_down": L0_ffn_sw_down,
    }
    arrays = {"in_" + n: np.ascontiguousarray(a) for n, a in arrays.items()}
    nc = bacc.Bacc("TRN2", target_bir_lowering=False, num_devices=1)
    args = [nc.dram_tensor(n, a.shape, mybir.dt.from_np(a.dtype), kind="ExternalInput").ap() for n, a in arrays.items()]
    out = nc.dram_tensor("out", x.shape, mybir.dt.float32, kind="ExternalOutput").ap()
    build(nc, *args, out)
    return run_bass_kernel_spmd(nc, [arrays], core_ids=[0]).results[0]["out"]
```
